# Optimizing a Trainium2 kernel written in Bass

```python
import numpy as np
import jax
import jax.numpy as jnp

def _softmax(x, axis=-1):
    return jax.nn.softmax(x, axis=axis)

def _gelu(x):
    return jax.nn.gelu(x, approximate=True)

def _silu(x):
    return jax.nn.silu(x)

def _sigmoid(x):
    return jax.nn.sigmoid(x)

def _layernorm(x, axis=-1, eps=1e-05):
    m = jnp.mean(x, axis=axis, keepdims=True)
    v = jnp.var(x, axis=axis, keepdims=True)
    return (x - m) / jnp.sqrt(v + eps)

def _scatter_add(tgt, idx, src, axis=0):
    return tgt.at[idx].add(src)

def _segment_sum(src, seg, n):
    return jax.ops.segment_sum(src, seg, n)
kernel_name = 'mk_dlrm_tower_d1_rec_r8_9ff4fd'

def setup_inputs(seed: int=0):
    np.random.seed(seed)
    _w = jnp.asarray

    def _rec_inputs():
        import jax
        import jax.numpy as jnp
        _tk = jax.random.key(seed)
        dense_ctx = jax.random.normal(jax.random.fold_in(_tk, 190), (1024, 16), jnp.float32)
        ids = jnp.stack([jax.random.randint(jax.random.fold_in(_tk, 200 + f), (1024,), 0, v, jnp.int32) for f, v in enumerate([1250, 12500, 1250, 12500, 1250, 12500, 12500, 1000, 1250, 125000, 1000, 1000, 125000, 12500, 125000, 1000, 12500, 1000, 1000, 1250, 12500, 1000, 12500, 1250, 125000, 12500, 1000, 1000, 12500, 125000, 12500, 125000])], axis=1)
        tbl_0 = 0.05 * jax.random.normal(jax.random.fold_in(_tk, 500 + 0), (1250, 16), jnp.float32)
        tbl_1 = 0.05 * jax.random.normal(jax.random.fold_in(_tk, 500 + 1), (12500, 16), jnp.float32)
        tbl_2 = 0.05 * jax.random.normal(jax.random.fold_in(_tk, 500 + 2), (1250, 16), jnp.float32)
        tbl_3 = 0.05 * jax.random.normal(jax.random.fold_in(_tk, 500 + 3), (12500, 16), jnp.float32)
        tbl_4 = 0.05 * jax.random.normal(jax.random.fold_in(_tk, 500 + 4), (1250, 16), jnp.float32)
        tbl_5 = 0.05 * jax.random.normal(jax.random.fold_in(_tk, 500 + 5), (12500, 16), jnp.float32)
        tbl_6 = 0.05 * jax.random.normal(jax.random.fold_in(_tk, 500 + 6), (12500, 16), jnp.float32)
        tbl_7 = 0.05 * jax.random.normal(jax.random.fold_in(_tk, 500 + 7), (1000, 16), jnp.float32)
        tbl_8 = 0.05 * jax.random.normal(jax.random.fold_in(_tk, 500 + 8), (1250, 16), jnp.float32)
        tbl_9 = 0.05 * jax.random.normal(jax.random.fold_in(_tk, 500 + 9), (125000, 16), jnp.float32)
        tbl_10 = 0.05 * jax.random.normal(jax.random.fold_in(_tk, 500 + 10), (1000, 16), jnp.float32)
        tbl_11 = 0.05 * jax.random.normal(jax.random.fold_in(_tk, 500 + 11), (1000, 16), jnp.float32)
        tbl_12 = 0.05 * jax.random.normal(jax.random.fold_in(_tk, 500 + 12), (125000, 16), jnp.float32)
        tbl_13 = 0.05 * jax.random.normal(jax.random.fold_in(_tk, 500 + 13), (12500, 16), jnp.float32)
        tbl_14 = 0.05 * jax.random.normal(jax.random.fold_in(_tk, 500 + 14), (125000, 16), jnp.float32)
        tbl_15 = 0.05 * jax.random.normal(jax.random.fold_in(_tk, 500 + 15), (1000, 16), jnp.float32)
        tbl_16 = 0.05 * jax.random.normal(jax.random.fold_in(_tk, 500 + 16), (12500, 16), jnp.float32)
        tbl_17 = 0.05 * jax.random.normal(jax.random.fold_in(_tk, 500 + 17), (1000, 16), jnp.float32)
        tbl_18 = 0.05 * jax.random.normal(jax.random.fold_in(_tk, 500 + 18), (1000, 16), jnp.float32)
        tbl_19 = 0.05 * jax.random.normal(jax.random.fold_in(_tk, 500 + 19), (1250, 16), jnp.float32)
        tbl_20 = 0.05 * jax.random.normal(jax.random.fold_in(_tk, 500 + 20), (12500, 16), jnp.float32)
        tbl_21 = 0.05 * jax.random.normal(jax.random.fold_in(_tk, 500 + 21), (1000, 16), jnp.float32)
        tbl_22 = 0.05 * jax.random.normal(jax.random.fold_in(_tk, 500 + 22), (12500, 16), jnp.float32)
        tbl_23 = 0.05 * jax.random.normal(jax.random.fold_in(_tk, 500 + 23), (1250, 16), jnp.float32)
        tbl_24 = 0.05 * jax.random.normal(jax.random.fold_in(_tk, 500 + 24), (125000, 16), jnp.float32)
        tbl_25 = 0.05 * jax.random.normal(jax.random.fold_in(_tk, 500 + 25), (12500, 16), jnp.float32)
        tbl_26 = 0.05 * jax.random.normal(jax.random.fold_in(_tk, 500 + 26), (1000, 16), jnp.float32)
        tbl_27 = 0.05 * jax.random.normal(jax.random.fold_in(_tk, 500 + 27), (1000, 16), jnp.float32)
        tbl_28 = 0.05 * jax.random.normal(jax.random.fold_in(_tk, 500 + 28), (12500, 16), jnp.float32)
        tbl_29 = 0.05 * jax.random.normal(jax.random.fold_in(_tk, 500 + 29), (125000, 16), jnp.float32)
        tbl_30 = 0.05 * jax.random.normal(jax.random.fold_in(_tk, 500 + 30), (12500, 16), jnp.float32)
        tbl_31 = 0.05 * jax.random.normal(jax.random.fold_in(_tk, 500 + 31), (125000, 16), jnp.float32)
        _rk = jax.random.fold_in(_tk, 7)
        W_top1 = 0.0693375 * jax.random.normal(jax.random.fold_in(_tk, 801), (208, 512), jnp.float32)
        W_top2 = 0.0441942 * jax.random.normal(jax.random.fold_in(_tk, 802), (512, 256), jnp.float32)
        W_top3 = 0.0625 * jax.random.normal(jax.random.fold_in(_tk, 803), (256, 1), jnp.float32)
        b_top1 = jnp.zeros((512,), jnp.float32)
        b_top2 = jnp.zeros((256,), jnp.float32)
        return (dense_ctx, ids, tbl_0, tbl_1, tbl_2, tbl_3, tbl_4, tbl_5, tbl_6, tbl_7, tbl_8, tbl_9, tbl_10, tbl_11, tbl_12, tbl_13, tbl_14, tbl_15, tbl_16, tbl_17, tbl_18, tbl_19, tbl_20, tbl_21, tbl_22, tbl_23, tbl_24, tbl_25, tbl_26, tbl_27, tbl_28, tbl_29, tbl_30, tbl_31, W_top1, b_top1, W_top2, b_top2, W_top3)
    dense_ctx, ids, tbl_0, tbl_1, tbl_2, tbl_3, tbl_4, tbl_5, tbl_6, tbl_7, tbl_8, tbl_9, tbl_10, tbl_11, tbl_12, tbl_13, tbl_14, tbl_15, tbl_16, tbl_17, tbl_18, tbl_19, tbl_20, tbl_21, tbl_22, tbl_23, tbl_24, tbl_25, tbl_26, tbl_27, tbl_28, tbl_29, tbl_30, tbl_31, W_top1, b_top1, W_top2, b_top2, W_top3 = _rec_inputs()

    def _L0_rec_setup():
        import jax, jax.numpy as jnp
        import numpy as np
        B, M, D = (2048, 32, 16)
        LAYERS = [64, 64, 64]
        key = jax.random.key(seed)
        ks = jax.random.split(key, 4)
        inp = {'embeddings': jax.random.normal(ks[0], (B, M, D), dtype=jnp.float32)}
        hk_1 = M
        for i, hk in enumerate(LAYERS):
            scale = (2.0 / (M * hk_1 + hk)) ** 0.5
            inp[f'W{i}'] = jax.random.normal(ks[i + 1], (M, hk_1, hk), dtype=jnp.float32) * scale
            hk_1 = hk
        return inp
    _L0_rec_all = _L0_rec_setup()
    _L0_rec_in = {k: v for k, v in _L0_rec_all.items() if k in ('W0', 'W1', 'W2')}
    del _L0_rec_all
    return {'dense_ctx': dense_ctx, 'ids': ids, 'tbl_0': tbl_0, 'tbl_1': tbl_1, 'tbl_2': tbl_2, 'tbl_3': tbl_3, 'tbl_4': tbl_4, 'tbl_5': tbl_5, 'tbl_6': tbl_6, 'tbl_7': tbl_7, 'tbl_8': tbl_8, 'tbl_9': tbl_9, 'tbl_10': tbl_10, 'tbl_11': tbl_11, 'tbl_12': tbl_12, 'tbl_13': tbl_13, 'tbl_14': tbl_14, 'tbl_15': tbl_15, 'tbl_16': tbl_16, 'tbl_17': tbl_17, 'tbl_18': tbl_18, 'tbl_19': tbl_19, 'tbl_20': tbl_20, 'tbl_21': tbl_21, 'tbl_22': tbl_22, 'tbl_23': tbl_23, 'tbl_24': tbl_24, 'tbl_25': tbl_25, 'tbl_26': tbl_26, 'tbl_27': tbl_27, 'tbl_28': tbl_28, 'tbl_29': tbl_29, 'tbl_30': tbl_30, 'tbl_31': tbl_31, 'W_top1': W_top1, 'b_top1': b_top1, 'W_top2': W_top2, 'b_top2': b_top2, 'W_top3': W_top3, 'L0_rec_W0': _L0_rec_in['W0'], 'L0_rec_W1': _L0_rec_in['W1'], 'L0_rec_W2': _L0_rec_in['W2']}

def reference(dense_ctx, ids, tbl_0, tbl_1, tbl_2, tbl_3, tbl_4, tbl_5, tbl_6, tbl_7, tbl_8, tbl_9, tbl_10, tbl_11, tbl_12, tbl_13, tbl_14, tbl_15, tbl_16, tbl_17, tbl_18, tbl_19, tbl_20, tbl_21, tbl_22, tbl_23, tbl_24, tbl_25, tbl_26, tbl_27, tbl_28, tbl_29, tbl_30, tbl_31, W_top1, b_top1, W_top2, b_top2, W_top3, L0_rec_W0, L0_rec_W1, L0_rec_W2):
    import jax
    import jax.numpy as jnp

    def _L0_rec_ref(embeddings, W0, W1, W2):
        import jax, jax.numpy as jnp
        import numpy as np
        B, M, D = (2048, 32, 16)
        LAYERS = [64, 64, 64]
        x0 = embeddings
        xk = x0
        outs = []
        for W in (W0, W1, W2):
            xk = jax.nn.relu(jnp.einsum('bmd,bhd,mhk->bkd', x0, xk, W))
            outs.append(jnp.sum(xk, axis=2))
        return jnp.concatenate(outs, axis=1)
    e = jnp.stack([tbl_0[ids[:, 0]], tbl_1[ids[:, 1]], tbl_2[ids[:, 2]], tbl_3[ids[:, 3]], tbl_4[ids[:, 4]], tbl_5[ids[:, 5]], tbl_6[ids[:, 6]], tbl_7[ids[:, 7]], tbl_8[ids[:, 8]], tbl_9[ids[:, 9]], tbl_10[ids[:, 10]], tbl_11[ids[:, 11]], tbl_12[ids[:, 12]], tbl_13[ids[:, 13]], tbl_14[ids[:, 14]], tbl_15[ids[:, 15]], tbl_16[ids[:, 16]], tbl_17[ids[:, 17]], tbl_18[ids[:, 18]], tbl_19[ids[:, 19]], tbl_20[ids[:, 20]], tbl_21[ids[:, 21]], tbl_22[ids[:, 22]], tbl_23[ids[:, 23]], tbl_24[ids[:, 24]], tbl_25[ids[:, 25]], tbl_26[ids[:, 26]], tbl_27[ids[:, 27]], tbl_28[ids[:, 28]], tbl_29[ids[:, 29]], tbl_30[ids[:, 30]], tbl_31[ids[:, 31]]], axis=1)
    z = _L0_rec_ref(e, L0_rec_W0, L0_rec_W1, L0_rec_W2)
    z = z.reshape(z.shape[0], -1)
    h = jnp.concatenate([z, dense_ctx], axis=1)
    h = jnp.maximum(h @ W_top1 + b_top1, 0.0)
    h = jnp.maximum(h @ W_top2 + b_top2, 0.0)
    y = h @ W_top3
    return y

_drawn_inputs = setup_inputs


def setup_inputs(seed=0):
    import zlib

    import numpy as np

    out = dict(_drawn_inputs(seed))
    spreads = {'b_top1': (0.0, 2.0), 'b_top2': (0.0, 0.8)}
    factors = {'tbl_0': 8.0,
     'tbl_1': 8.0,
     'tbl_2': 8.0,
     'tbl_3': 8.0,
     'tbl_4': 8.0,
     'tbl_5': 8.0,
     'tbl_6': 8.0,
     'tbl_7': 8.0,
     'tbl_8': 8.0,
     'tbl_9': 8.0,
     'tbl_10': 8.0,
     'tbl_11': 8.0,
     'tbl_12': 8.0,
     'tbl_13': 8.0,
     'tbl_14': 8.0,
     'tbl_15': 8.0,
     'tbl_16': 8.0,
     'tbl_17': 8.0,
     'tbl_18': 8.0,
     'tbl_19': 8.0,
     'tbl_20': 8.0,
     'tbl_21': 8.0,
     'tbl_22': 8.0,
     'tbl_23': 8.0,
     'tbl_24': 8.0,
     'tbl_25': 8.0,
     'tbl_26': 8.0,
     'tbl_27': 8.0,
     'tbl_28': 8.0,
     'tbl_29': 8.0,
     'tbl_30': 8.0,
     'tbl_31': 8.0,
     'L0_rec_W0': 3.532,
     'L0_rec_W1': 8.0,
     'L0_rec_W2': 8.0,
     'dense_ctx': 7.178}
    for name, (base, spread) in spreads.items():
        noise = np.random.default_rng([zlib.crc32(name.encode()), seed]).standard_normal(out[name].shape)
        drawn = base * np.exp(spread * noise) if base else spread * noise
        out[name] = jnp.asarray(drawn.astype(out[name].dtype))
    for name, factor in factors.items():
        out[name] = (out[name] * factor).astype(out[name].dtype)
    return out
```

```python
from contextlib import ExitStack

import numpy as np

import concourse.bass as bass
from concourse import mybir

F32 = mybir.dt.float32
BF16 = mybir.dt.bfloat16
I32 = mybir.dt.int32
ALU = mybir.AluOpType
ACT = mybir.ActivationFunctionType

P = 128
HALF = 64
ROWS = 1024
M = 32
D = 16
K = 64
PARTS = 3
CTX = 16
BLOCKS = ROWS // P
UNIT_D = 4
UNIT = UNIT_D * P
Q = UNIT // 2
PAIRS = 2
TILES = M // 2
GROUP = 4
GROUPS = TILES // GROUP
SHIFTS = M // 2
Z_BUFS = 3
STEP_GROUPS = 4 * GROUPS + 2
SLOTS_0 = 1 + GROUP
SLOTS = 2 * SLOTS_0 + 2 * TILES
LATE_SLOT = 2 * SLOTS_0 + TILES + 4
TURN_BEHIND = 2
SPLIT_STEPS = 4
F_TOP1, F_TOP2 = 512, 256


def selections():
    one = np.uint16(0x3F80)
    sel = np.zeros((PARTS, M, 1 + GROUP + TILES, P), np.uint16)
    for p in range(P):
        sel[:, p % M, 0, p] = one
        for j in range(GROUP):
            sel[:, (p % M + GROUP * j + p // M + 1) % M, 1 + j, p] = one
        for t in range(TILES):
            sel[:, 2 * t + p // HALF, 1 + GROUP + t, p] = one
    return sel.reshape(PARTS * M, -1)


def identity():
    return (np.eye(P) * 0x3F80).astype(np.uint16)


def slot_plan():
    plan = [0, 0, 0, 2, 3, 3, 2] + [3] * 11
    plan[-1] -= sum(plan) - SLOTS
    return plan


def build(nc, a):
    plan = slot_plan()

    with ExitStack() as ctx:
        def sb(name, shape, dt):
            return ctx.enter_context(nc.sbuf_tensor(name, shape, dt))

        def psum(name, shape, dt):
            return ctx.enter_context(nc.psum_tensor(name, shape, dt))

        def sem(name):
            return ctx.enter_context(nc.semaphore(name))

        rep = sb("rep", [P, 2, 2, TILES, UNIT], F32)
        z = sb("z", [P, Z_BUFS, GROUP, UNIT], F32)
        w1 = sb("w1", [P, TILES, K], F32)
        w2 = sb("w2", [P, TILES, K], F32)
        w0 = sb("w0", [P, GROUP, K], F32)
        w0_other = sb("w0_other", [P, GROUP, K], F32)
        w0_square = sb("w0_square", [P, K], F32)
        sel = sb("sel", [PARTS * M, 1 + GROUP + TILES, P], BF16)
        ident = sb("ident", [P, P], BF16)
        ids = sb("ids", [P, M], I32)
        emb = sb("emb", [P, M * D], F32)
        rest = sb("rest", [P, M * D], F32)
        parts = sb("parts", [P, D, PARTS, M], BF16)
        partsT = sb("partsT", [PARTS * M, 2 * UNIT], BF16)
        relu_out = [sb(f"relu_out{l}", [P, 2, Q], F32) for l in range(3)]
        zsum_a = sb("zsum_a", [P, 3, Q], F32)
        zsum_b = sb("zsum_b", [P, Q], F32)
        zsum_c = sb("zsum_c", [P, 3, Q], F32)
        zsum = sb("zsum", [P, 3, ROWS], F32)

        xin = [psum(f"xin{u}", [P, UNIT], F32) for u in range(2)]
        acc = [psum(f"acc12_{u}", [P, 512], F32) for u in range(2)]
        acc0 = psum("acc0", [P, 2, Q], F32)
        ring = [psum(f"ring{r}", [P, UNIT], F32) for r in range(2)]
        turned = psum("turned", [PARTS * M, 2 * UNIT], BF16)

        const_in = sem("const_in")
        w0_cleared, w0_in, w0_summed = sem("w0_cleared"), sem("w0_in"), sem("w0_summed")
        w12_in = sem("w12_in")
        ids_in, gathered, split = sem("ids_in"), sem("gathered"), sem("split")
        pool_passed = sem("pool_passed")
        turned_done, partsT_ready = sem("turned_done"), sem("partsT_ready")
        slot_done, slot_copied, squares_ready = sem("slot_done"), sem("slot_copied"), sem("squares_ready")
        z_ready, z_used = sem("z_ready"), sem("z_used")
        xin_ready = [sem(f"xin{u}_ready") for u in range(2)]
        relu_ready = [sem(f"relu{l}_ready") for l in range(3)]
        relu_used = [sem(f"relu{l}_used") for l in range(3)]
        zsum_step = [sem(f"zsum{l}_step") for l in range(3)]
        top_in, top_shifted, top_packed = sem("top_in"), sem("top_shifted"), sem("top_packed")
        top_done, top_copied, out_done = sem("top_done"), sem("top_copied"), sem("out_done")

        def wait(eng, s, value):
            if not isinstance(value, int) or value > 0:
                eng.wait_ge(s, value)

        def x0_rep(par, u):
            return rep[:, par, 1, GROUP + u, :]

        def x0_square(par, u):
            return rep[:, par, 1, GROUP + 2 + u, :]

        def x0_shifts(par, u):
            return rep[:, par, 1, 2 * GROUP + GROUP * u:3 * GROUP + GROUP * u, :]

        def groups(b, j, last=False):
            p = b * PAIRS + j
            order = [(1, u, k) for u in range(2) for k in range(GROUPS)]
            if not last:
                order += [(0, u, 0) for u in range(2)]
            order += [(2, u, k) for u in range(2) for k in range(GROUPS)]
            return [(p * STEP_GROUPS + 2 + g, (2 + g) % Z_BUFS, l, u, k) for g, (l, u, k) in enumerate(order)]

        first_groups = [(u, u, 0, u, 0) for u in range(2)]

        def behind(g):
            return range(sum(plan[:g]), sum(plan[:g + 1]))

        spare = rep[:, 0].rearrange("p u t n -> p (u t n)")
        taken = [0]

        def spare_of(c, n):
            v = spare[:, taken[0]:taken[0] + c * n]
            taken[0] += c * n
            return v.rearrange("p (c n) -> p c n", c=c)

        top1 = spare_of(2, F_TOP1)
        top2 = spare_of(F_TOP1 // P, F_TOP2)
        top3 = spare_of(1, F_TOP2 // P)
        bias1 = spare_of(1, F_TOP1 // P)
        bias2 = spare_of(1, F_TOP2 // P)
        shifted = spare_of(3, ROWS)
        packed = spare_of(2, ROWS)
        hid1 = spare_of(F_TOP1 // P, ROWS)
        hid2 = spare_of(F_TOP2 // P, ROWS)
        y = spare_of(1, ROWS)

        halves = [slice(n * 512, (n + 1) * 512) for n in range(ROWS // 512)]
        top_steps = [(l, c, cols) for l, tiles in ((1, F_TOP1 // P), (2, F_TOP2 // P), (3, 1))
                     for cols in halves for c in range(tiles)]

        block = ctx.enter_context(nc.Block())

        @block.sync
        def _(sp):
            sp.dma_start(ids[:], a["ids"][0:P, :]).then_inc(ids_in, 16)
            sp.dma_start(ident[:], a["identity"].bitcast(BF16)).then_inc(const_in, 16)
            sp.dma_start(sel[:], a["selections"].bitcast(BF16).rearrange("k (s p) -> k s p", p=P)).then_inc(const_in, 16)
            sp.dma_start(w0[:], a["w0_mh"].rearrange("(j p) k -> p j k", p=P)).then_inc(w0_in, 16)
            sp.dma_start(w0_other[:], a["w0_hm"].rearrange("(j p) k -> p j k", p=P)).then_inc(w0_in, 16)
            sp.wait_ge(w0_cleared, 1)
            sp.dma_start(w0_square[0:M, :], a["w0_mm"]).then_inc(w0_in, 16)
            sp.dma_start(w1[:], a["L0_rec_W1"].rearrange("(t m) h k -> (m h) t k", m=2)).then_inc(w12_in, 16)
            sp.dma_start(w2[:], a["L0_rec_W2"].rearrange("(t m) h k -> (m h) t k", m=2)).then_inc(w12_in, 16)
            with sp.Fori(1, BLOCKS) as b:
                sp.wait_ge(gathered, b * (16 * M))
                sp.dma_start(ids[:], a["ids"][bass.ds(b * P, P), :]).then_inc(ids_in, 16)
            sp.wait_ge(z_ready, (BLOCKS * PAIRS - 1) * STEP_GROUPS + 2)
            sp.dma_start(top1[:, 0, :], a["W_top1"][0:P, :]).then_inc(top_in, 16)
            sp.dma_start(top1[0:K + CTX, 1, :], a["W_top1"][P:3 * K + CTX, :]).then_inc(top_in, 16)
            sp.dma_start(top2, a["W_top2"].rearrange("(c p) n -> p c n", p=P)).then_inc(top_in, 16)
            sp.dma_start(top3[:, 0, :], a["top3"]).then_inc(top_in, 16)
            sp.dma_start(bias1[:, 0, :], a["bias1"]).then_inc(top_in, 16)
            sp.dma_start(bias2[:, 0, :], a["bias2"]).then_inc(top_in, 16)
            sp.dma_start(packed[K:K + CTX, 1, :], a["ctxT"]).then_inc(top_in, 16)
            sp.wait_ge(top_copied, len(top_steps))
            sp.dma_start(a["out"].rearrange("b o -> o b"), y[0:1, 0, :]).then_inc(out_done, 16)
            sp.wait_ge(out_done, 16)

        @block.gpsimd
        def _(pool):
            pool.memset(w0_square[:], 0.0).then_inc(w0_cleared, 1)

            def alone():
                pool.sem_inc(pool_passed, 1)

            def gather(b):
                wait(pool, ids_in, (b + 1) * 16)
                wait(pool, split, b * SPLIT_STEPS)
                alone()
                for m in range(M):
                    pool.indirect_dma_start(emb[:, m * D:(m + 1) * D], None, a[f"tbl_{m}"],
                                            bass.IndirectOffsetOnAxis(ids[:, m:m + 1], 0)).then_inc(gathered, 16)

            def split_parts(b):
                src = emb[:].rearrange("p (m d) -> p m d", d=D)
                rst = rest[:].rearrange("p (m d) -> p m d", d=D)
                part = [parts[:, :, i, :].rearrange("p d m -> p m d") for i in range(PARTS)]
                wait(pool, gathered, (b + 1) * (16 * M))
                wait(pool, turned_done, b * PAIRS)
                alone()
                pool.tensor_copy(part[0], src).then_inc(split, 1)
                pool.wait_ge(split, b * SPLIT_STEPS + 1)
                pool.tensor_tensor(rst, src, part[0], ALU.subtract).then_inc(split, 1)
                pool.wait_ge(split, b * SPLIT_STEPS + 2)
                alone()
                pool.tensor_copy(part[1], rst).then_inc(split, 1)
                pool.wait_ge(split, b * SPLIT_STEPS + 3)
                pool.tensor_tensor(part[2], rst, part[1], ALU.subtract).then_inc(split, 1)

            def add_up(l, b, j):
                r = relu_out[l]
                pool.wait_ge(relu_ready[l], (b * PAIRS + (j + 1)) * (1 if l == 0 else 2))
                if j == 0:
                    pool.tensor_tensor(zsum_a[:, l], r[:, 0], r[:, 1], ALU.add).then_inc(relu_used[l], 1)
                    return
                pool.tensor_tensor(zsum_b[:], r[:, 0], r[:, 1], ALU.add).then_inc(relu_used[l], 1)
                pool.wait_ge(relu_used[l], b * PAIRS + 2)
                wait(pool, zsum_step[l], b * 2)
                pool.tensor_tensor(zsum_c[:, l], zsum_a[:, l], zsum_b[:], ALU.add).then_inc(zsum_step[l], 1)
                pool.wait_ge(zsum_step[l], b * 2 + 1)
                pool.tensor_tensor(zsum[:, l, bass.ds(b * P, P)], zsum_c[:, l, 0:P], zsum_c[:, l, P:Q],
                                   ALU.add).then_inc(zsum_step[l], 1)

            pool.wait_ge(w0_in, 48)
            last = (SHIFTS % GROUP or GROUP) - 1
            pool.tensor_tensor(w0[:, 0:GROUP - 1], w0[:, 0:GROUP - 1], w0_other[:, 0:GROUP - 1], ALU.add).then_inc(w0_summed, 1)
            pool.tensor_tensor(w0[0:M * last, GROUP - 1], w0[0:M * last, GROUP - 1], w0_other[0:M * last, GROUP - 1],
                               ALU.add).then_inc(w0_summed, 1)

            def body(b, last=False):
                if not last:
                    gather(b + 1)
                add_up(1, b, 0)
                if not last:
                    split_parts(b + 1)
                add_up(0, b, 1)
                add_up(2, b, 0)
                add_up(1, b, 1)
                if not last:
                    add_up(0, b + 1, 0)
                add_up(2, b, 1)

            gather(0)
            split_parts(0)
            add_up(0, 0, 0)
            body(0)
            with pool.Fori(1, BLOCKS - 1) as b:
                body(b)
            body(BLOCKS - 1, last=True)

        @block.tensor
        def _(pe):
            def transposes(b, j):
                pe.wait_ge(split, (b + 1) * SPLIT_STEPS)
                wait(pe, partsT_ready, b * PAIRS + j)
                for d in range(2 * UNIT_D):
                    mm = pe.transpose(turned[:, d * P:(d + 1) * P],
                                      parts[:, 2 * UNIT_D * j + d].rearrange("p c m -> p (c m)"), ident[:])
                mm.then_inc(turned_done, 1)

            def slot(p, s):
                if s == 0:
                    pe.wait_ge(partsT_ready, p + 1)
                if s < 2 * SLOTS_0:
                    u, which = divmod(s, SLOTS_0)
                else:
                    u, which = divmod(s - 2 * SLOTS_0, TILES)
                    which += SLOTS_0
                wait(pe, slot_copied, p * SLOTS + (s - 1))
                pe.matmul(ring[s % 2][:], sel[:, which, :], partsT[:, u * UNIT:(u + 1) * UNIT],
                          start=True, stop=True).then_inc(slot_done, 1)

            def products(b, j, group):
                n, buf, l, u, k = group
                p = b * PAIRS + j
                pe.wait_ge(z_ready, n + 1)
                sums = acc0[:, u] if l == 0 else acc[u][:, 0:Q]
                if l == 0 and u == 0:
                    wait(pe, xin_ready[1], 2 * p + 1)
                if l == 1 and k == 0:
                    wait(pe, relu_ready[2], 2 * p + (u - 1))
                if l == 2 and k == 0:
                    pe.wait_ge(xin_ready[u], 2 * p + 2)
                if l == 0:
                    pe.wait_ge(squares_ready, 2 * p + (2 + u + 1))
                    square = x0_square(1 - j, u)
                    for q in range(2):
                        pe.matmul(sums[HALF * q:HALF * (q + 1), :], w0_square[:], square[:, q * Q:(q + 1) * Q],
                                  start=True, stop=False)
                w = (w0, w1, w2)[l]
                ends = l == 0 or k == GROUPS - 1
                for t in range(GROUP):
                    for q in range(2):
                        mm = pe.matmul(sums[HALF * q:HALF * (q + 1), :], w[:, k * GROUP + t, :],
                                       z[:, buf, t, q * Q:(q + 1) * Q],
                                       start=l > 0 and k == 0 and t == 0, stop=ends and t == GROUP - 1)
                mm.then_inc(z_used, 1)

            def pair(b, j, last=False):
                nb, nj = (b, 1) if j == 0 else (b + 1, 0)
                for g, group in enumerate(groups(b, j, last)):
                    products(b, j, group)
                    if not last:
                        if g == TURN_BEHIND:
                            transposes(nb, nj)
                        for s in behind(g):
                            slot(b * PAIRS + (j + 1), s)

            pe.wait_ge(const_in, 32)
            transposes(0, 0)
            for s in range(SLOTS):
                slot(0, s)
                if s == 2 * SLOTS_0 - 1:
                    pe.wait_ge(w0_in, 48)
                    pe.wait_ge(w0_summed, 2)
                    for group in first_groups:
                        products(-1, 1, group)
            pe.wait_ge(w12_in, 32)
            for j in range(PAIRS):
                pair(0, j)
            with pe.Fori(1, BLOCKS - 1) as b:
                for j in range(PAIRS):
                    pair(b, j)
            pair(BLOCKS - 1, 0)
            pair(BLOCKS - 1, 1, last=True)

            def top_sum(step, m, terms):
                wait(pe, top_copied, step - 1)
                for i, (w, x) in enumerate(terms):
                    mm = pe.matmul(ring[step % 2][0:m, :], w, x, start=i == 0, stop=i == len(terms) - 1)
                mm.then_inc(top_done, 1)

            pe.wait_ge(top_in, 7 * 16)
            pe.wait_ge(top_packed, 3)
            for step, (layer, c, cols) in enumerate(top_steps):
                if layer == 1:
                    terms = [(top1[0:r, i, c * P:(c + 1) * P], packed[0:r, i, cols]) for i, r in enumerate((P, K + CTX))]
                elif layer == 2:
                    terms = [(top2[:, i, c * P:(c + 1) * P], hid1[:, i, cols]) for i in range(F_TOP1 // P)]
                else:
                    terms = [(top3[:, 0, i:i + 1], hid2[:, i, cols]) for i in range(F_TOP2 // P)]
                top_sum(step, P if layer < 3 else 1, terms)

        @block.scalar
        def _(act):
            def copy_parts(p):
                act.wait_ge(turned_done, p + 1)
                act.copy(partsT[:], turned[:]).then_inc(partsT_ready, 1)

            def copy_slot(p, par, s, layer0_used):
                if s == LATE_SLOT:
                    act.wait_ge(z_used, layer0_used)
                act.wait_ge(slot_done, p * SLOTS + (s + 1))
                bank = ring[s % 2][:]
                if s < 2 * SLOTS_0:
                    u, which = divmod(s, SLOTS_0)
                    if which == 0:
                        act.activation(x0_square(par, u), bank, ACT.Square).then_inc(squares_ready, 1)
                        out = x0_rep(par, u)
                    else:
                        out = x0_shifts(par, u)[:, which - 1]
                else:
                    u, t = divmod(s - 2 * SLOTS_0, TILES)
                    out = rep[:, par, u, t, :]
                act.copy(out, bank).then_inc(slot_copied, 1)

            def next_input(u, sums):
                for q in range(2):
                    for half in range(2):
                        ins = act.activation(xin[u][HALF * half:HALF * (half + 1), q * Q:(q + 1) * Q],
                                             sums[HALF * q:HALF * (q + 1)], ACT.Relu)
                ins.then_inc(xin_ready[u], 1)

            def evacuate(b, j, group):
                n, _, l, u, k = group
                p = b * PAIRS + j
                if l == 0 and u == 0 or l > 0 and k < GROUPS - 1:
                    return
                act.wait_ge(z_used, n + 1)
                if l == 0:
                    wait(act, relu_used[0], p + 1)
                    act.activation(relu_out[0][:], acc0[:], ACT.Relu).then_inc(relu_ready[0], 1)
                    return
                if u == 0:
                    wait(act, relu_used[l], p)
                act.activation(relu_out[l][:, u], acc[u][:, 0:Q], ACT.Relu).then_inc(relu_ready[l], 1)
                if l == 1:
                    next_input(u, acc[u][:, 0:Q])

            def pair(b, j, last=False):
                layer0_used = 0
                for g, group in enumerate(groups(b, j, last)):
                    evacuate(b, j, group)
                    n, _, l, u, k = group
                    if last:
                        continue
                    if l == 0:
                        layer0_used = n + 1
                    if l == 2 and k == GROUPS - 1:
                        next_input(u, acc0[:, u])
                    if g == TURN_BEHIND:
                        copy_parts(b * PAIRS + (j + 1))
                    for s in behind(g):
                        copy_slot(b * PAIRS + (j + 1), 1 - j, s, layer0_used)

            copy_parts(0)
            for s in range(SLOTS):
                copy_slot(0, 0, s, 2)
                if s == 2 * SLOTS_0 - 1:
                    for group in first_groups:
                        evacuate(-1, 1, group)
                    for u in range(2):
                        next_input(u, acc0[:, u])
            for j in range(PAIRS):
                pair(0, j)
            with act.Fori(1, BLOCKS - 1) as b:
                for j in range(PAIRS):
                    pair(b, j)
            pair(BLOCKS - 1, 0)
            pair(BLOCKS - 1, 1, last=True)

            for l, (to, of) in enumerate(((0, 1), (1, 0), (0, 1))):
                act.wait_ge(zsum_step[l], 2 * BLOCKS)
                act.copy(shifted[HALF * to:HALF * (to + 1), l, :], zsum[HALF * of:HALF * (of + 1), l, :]).then_inc(top_shifted, 1)
            act.wait_ge(top_in, 7 * 16)
            for step, (layer, c, cols) in enumerate(top_steps):
                act.wait_ge(top_done, step + 1)
                bank = ring[step % 2]
                if layer == 1:
                    ins = act.activation(hid1[:, c, cols], bank[:], ACT.Relu, bias=bias1[:, 0, c:c + 1])
                elif layer == 2:
                    ins = act.activation(hid2[:, c, cols], bank[:], ACT.Relu, bias=bias2[:, 0, c:c + 1])
                else:
                    ins = act.copy(y[0:1, 0, cols], bank[0:1, :])
                ins.then_inc(top_copied, 1)

        @block.vector
        def _(dve):
            def multiply(b, j, group):
                n, buf, l, u, k = group
                p = b * PAIRS + j
                wait(dve, z_used, n - (Z_BUFS - 1))
                if l == 0:
                    dve.wait_ge(slot_copied, (p + 1) * SLOTS + SLOTS_0 * (u + 1))
                    tiles, other = x0_shifts(1 - j, u), x0_rep(1 - j, u)
                else:
                    if k == 0:
                        dve.wait_ge(xin_ready[u], 2 * p + l)
                    if l == 1:
                        dve.wait_ge(slot_copied, p * SLOTS + (2 * SLOTS_0 + TILES * u + GROUP * (k + 1)))
                    tiles, other = rep[:, j, u, GROUP * k:GROUP * (k + 1), :], xin[u][:]
                dve.tensor_tensor(z[:, buf], tiles, other.unsqueeze(1).to_broadcast([P, GROUP, UNIT]),
                                  ALU.mult).then_inc(z_ready, 1)

            for group in first_groups:
                multiply(-1, 1, group)
            for j in range(PAIRS):
                for group in groups(0, j):
                    multiply(0, j, group)
            with dve.Fori(1, BLOCKS - 1) as b:
                for j in range(PAIRS):
                    for group in groups(b, j):
                        multiply(b, j, group)
            for j in range(PAIRS):
                for group in groups(BLOCKS - 1, j, j == PAIRS - 1):
                    multiply(BLOCKS - 1, j, group)

            for l, (h, c) in enumerate(((0, 0), (1, 0), (0, 1))):
                dve.wait_ge(top_shifted, l + 1)
                rows = slice(HALF * h, HALF * (h + 1))
                dve.tensor_tensor(packed[rows, c, :], zsum[rows, l, :], shifted[rows, l, :],
                                  ALU.add).then_inc(top_packed, 1)


def kernel(**inputs):
    import concourse.bacc as bacc
    from concourse.bass_utils import run_bass_kernel_spmd

    w0 = inputs["L0_rec_W0"]
    m = np.arange(M)
    shift = np.arange(1, SHIFTS + 1)[:, None]
    arrays = {
        "ids": inputs["ids"],
        "selections": selections(),
        "identity": identity(),
        "w0_mh": w0[m, (m + shift) % M].reshape(SHIFTS * M, K),
        "w0_hm": w0[(m + shift) % M, m].reshape(SHIFTS * M, K),
        "w0_mm": w0[m, m],
        "L0_rec_W1": inputs["L0_rec_W1"],
        "L0_rec_W2": inputs["L0_rec_W2"],
        "W_top1": inputs["W_top1"],
        "W_top2": inputs["W_top2"],
        "top3": inputs["W_top3"].reshape(F_TOP2 // P, P).T,
        "bias1": inputs["b_top1"].reshape(F_TOP1 // P, P).T,
        "bias2": inputs["b_top2"].reshape(F_TOP2 // P, P).T,
        "ctxT": inputs["dense_ctx"].T,
    }
    arrays.update({f"tbl_{i}": inputs[f"tbl_{i}"] for i in range(M)})
    arrays = {name: np.ascontiguousarray(x) for name, x in arrays.items()}

    nc = bacc.Bacc("TRN2", target_bir_lowering=False, num_devices=1)
    aps = {name: nc.dram_tensor("in_" + name, x.shape, mybir.dt.from_np(x.dtype), kind="ExternalInput").ap()
           for name, x in arrays.items()}
    aps["out"] = nc.dram_tensor("out", (ROWS, 1), F32, kind="ExternalOutput").ap()
    build(nc, aps)
    result = run_bass_kernel_spmd(nc, [{"in_" + name: x for name, x in arrays.items()}], core_ids=[0])
    return result.results[0]["out"]
```

```python
from contextlib import ExitStack

import numpy as np

import concourse.bass as bass
from concourse import mybir

F32 = mybir.dt.float32
BF16 = mybir.dt.bfloat16
I32 = mybir.dt.int32
ALU = mybir.AluOpType
ACT = mybir.ActivationFunctionType

P = 128
HALF = 64
ROWS = 1024
M = 32
D = 16
K = 64
PARTS = 3
CTX = 16
BLOCKS = ROWS // P
UNIT_D = 4
UNIT = UNIT_D * P
Q = UNIT // 2
PAIRS = 2
TILES = M // 2
GROUP = 4
GROUPS = TILES // GROUP
SHIFTS = M // 2
Z_BUFS = 3
RING = 3
STEP_GROUPS = 4 * GROUPS + 2
SLOTS_0 = 1 + GROUP
SLOTS = 2 * SLOTS_0 + 2 * TILES
LATE_SLOT = 2 * SLOTS_0 + TILES + 4
TURN_BEHIND = 0
SLOT_BEHIND = (0, 1, 3)
FIRST_LAYER0 = 2 * SLOTS_0 + GROUP + 1
TOP_BEHIND = 2
SPLIT_STEPS = 4
F_TOP1, F_TOP2 = 512, 256


def selections():
    one = np.uint16(0x3F80)
    sel = np.zeros((PARTS, M, 1 + GROUP + TILES, P), np.uint16)
    for p in range(P):
        sel[:, p % M, 0, p] = one
        for j in range(GROUP):
            sel[:, (p % M + GROUP * j + p // M + 1) % M, 1 + j, p] = one
        for t in range(TILES):
            sel[:, 2 * t + p // HALF, 1 + GROUP + t, p] = one
    return sel.reshape(PARTS * M, -1)


def identity():
    return (np.eye(P) * 0x3F80).astype(np.uint16)


def slot_plan():
    return [0] + [2, 3, 2, 3, 2] + [3, 2] * 5 + [3, 2][:2]


def build(nc, a):
    plan = slot_plan()

    with ExitStack() as ctx:
        def sb(name, shape, dt):
            return ctx.enter_context(nc.sbuf_tensor(name, shape, dt))

        def psum(name, shape, dt):
            return ctx.enter_context(nc.psum_tensor(name, shape, dt))

        def sem(name):
            return ctx.enter_context(nc.semaphore(name))

        rep = sb("rep", [P, 2, 2, TILES, UNIT], F32)
        z = sb("z", [P, Z_BUFS, GROUP, UNIT], F32)
        w1 = sb("w1", [P, TILES, K], F32)
        w2 = sb("w2", [P, TILES, K], F32)
        w0 = sb("w0", [P, GROUP, K], F32)
        w0_other = sb("w0_other", [P, GROUP, K], F32)
        w0_square = sb("w0_square", [P, K], F32)
        sel = sb("sel", [PARTS * M, 1 + GROUP + TILES, P], BF16)
        ident = sb("ident", [P, P], BF16)
        ids = sb("ids", [P, M], I32)
        emb = sb("emb", [P, M * D], F32)
        rest = sb("rest", [P, M * D], F32)
        parts = sb("parts", [P, D, PARTS, M], BF16)
        partsT = sb("partsT", [PARTS * M, 2 * UNIT], BF16)
        relu_out = [sb(f"relu_out{l}", [P, 2, Q], F32) for l in range(3)]
        zsum_a = sb("zsum_a", [P, 3, Q], F32)
        zsum_b = sb("zsum_b", [P, Q], F32)
        zsum_c = sb("zsum_c", [P, 3, Q], F32)
        zsum = sb("zsum", [P, 3, ROWS], F32)

        xin = [psum(f"xin{u}", [P, UNIT], F32) for u in range(2)]
        acc = [psum(f"acc12_{u}", [P, 512], F32) for u in range(2)]
        acc0 = psum("acc0", [P, 2, Q], F32)
        turned = acc0[0:PARTS * M].rearrange("p u n -> p (u n)").bitcast(BF16)
        ring = [psum(f"ring{r}", [P, UNIT], F32) for r in range(RING)]

        const_in = sem("const_in")
        w0_cleared, w0_in, w0_summed = sem("w0_cleared"), sem("w0_in"), sem("w0_summed")
        w12_in = sem("w12_in")
        ids_in, gathered, split = sem("ids_in"), sem("gathered"), sem("split")
        pool_passed = sem("pool_passed")
        turned_done, partsT_ready = sem("turned_done"), sem("partsT_ready")
        slot_done, slot_copied, squares_ready = sem("slot_done"), sem("slot_copied"), sem("squares_ready")
        z_ready, z_used = sem("z_ready"), sem("z_used")
        xin_ready = [sem(f"xin{u}_ready") for u in range(2)]
        relu_ready = [sem(f"relu{l}_ready") for l in range(3)]
        relu_used = [sem(f"relu{l}_used") for l in range(3)]
        zsum_step = [sem(f"zsum{l}_step") for l in range(3)]
        top_in, top_shifted, top_packed = sem("top_in"), sem("top_shifted"), sem("top_packed")
        top_done, top_copied, out_done = sem("top_done"), sem("top_copied"), sem("out_done")

        def wait(eng, s, value):
            if not isinstance(value, int) or value > 0:
                eng.wait_ge(s, value)

        def x0_rep(par, u):
            return rep[:, par, 1, GROUP + u, :]

        def x0_square(par, u):
            return rep[:, par, 1, GROUP + 2 + u, :]

        def x0_shifts(par, u):
            return rep[:, par, 1, 2 * GROUP + GROUP * u:3 * GROUP + GROUP * u, :]

        def groups(b, j, last=False):
            p = b * PAIRS + j
            order = [(1, u, k) for u in range(2) for k in range(GROUPS)]
            if not last:
                order += [(0, u, 0) for u in range(2)]
            order += [(2, u, k) for u in range(2) for k in range(GROUPS)]
            return [(p * STEP_GROUPS + 2 + g, (2 + g) % Z_BUFS, l, u, k) for g, (l, u, k) in enumerate(order)]

        first_groups = [(u, u, 0, u, 0) for u in range(2)]

        def first_slot(g):
            return sum(plan[:g])

        def behind(g):
            return range(first_slot(g), first_slot(g + 1))

        spare = rep[:, 0].rearrange("p u t n -> p (u t n)")
        taken = [0]

        def spare_of(c, n):
            v = spare[:, taken[0]:taken[0] + c * n]
            taken[0] += c * n
            return v.rearrange("p (c n) -> p c n", c=c)

        top1 = spare_of(2, F_TOP1)
        top2 = spare_of(F_TOP1 // P, F_TOP2)
        top3 = spare_of(1, F_TOP2 // P)
        bias1 = spare_of(1, F_TOP1 // P)
        bias2 = spare_of(1, F_TOP2 // P)
        shifted = spare_of(3, ROWS)
        packed = spare_of(2, ROWS)
        hid1 = spare_of(F_TOP1 // P, ROWS)
        hid2 = spare_of(F_TOP2 // P, ROWS)
        y = spare_of(1, ROWS)

        last_rows = ROWS - P
        ranges = [slice(0, 512), slice(512, last_rows), slice(last_rows, ROWS)]
        tiles = {1: F_TOP1 // P, 2: F_TOP2 // P, 3: 1}
        top_steps = []
        for together in ((0, 1), (2,)):
            for layer in (1, 2, 3):
                for r in together:
                    needed = [n + 1 for n, x in enumerate(top_steps) if x[0] == layer - 1 and x[2] == r]
                    top_steps += [(layer, c, r, max(needed, default=0)) for c in range(tiles[layer])]
        EARLY = len(top_steps) - sum(tiles.values())

        block = ctx.enter_context(nc.Block())

        @block.sync
        def _(sp):
            sp.dma_start(ids[:], a["ids"][0:P, :]).then_inc(ids_in, 16)
            sp.dma_start(ident[:], a["identity"].bitcast(BF16)).then_inc(const_in, 16)
            sp.dma_start(sel[:], a["selections"].bitcast(BF16).rearrange("k (s p) -> k s p", p=P)).then_inc(const_in, 16)
            sp.dma_start(w0[:], a["w0_mh"].rearrange("(j p) k -> p j k", p=P)).then_inc(w0_in, 16)
            sp.dma_start(w0_other[:], a["w0_hm"].rearrange("(j p) k -> p j k", p=P)).then_inc(w0_in, 16)
            sp.wait_ge(w0_cleared, 1)
            sp.dma_start(w0_square[0:M, :], a["w0_mm"]).then_inc(w0_in, 16)
            sp.dma_start(w1[:], a["L0_rec_W1"].rearrange("(t m) h k -> (m h) t k", m=2)).then_inc(w12_in, 16)
            sp.dma_start(w2[:], a["L0_rec_W2"].rearrange("(t m) h k -> (m h) t k", m=2)).then_inc(w12_in, 16)
            with sp.Fori(1, BLOCKS) as b:
                sp.wait_ge(gathered, b * (16 * M))
                sp.dma_start(ids[:], a["ids"][bass.ds(b * P, P), :]).then_inc(ids_in, 16)
            sp.wait_ge(z_ready, (BLOCKS * PAIRS - 1) * STEP_GROUPS + 2)
            sp.dma_start(top1[:, 0, :], a["W_top1"][0:P, :]).then_inc(top_in, 16)
            sp.dma_start(top1[0:K + CTX, 1, :], a["W_top1"][P:3 * K + CTX, :]).then_inc(top_in, 16)
            sp.dma_start(top2, a["W_top2"].rearrange("(c p) n -> p c n", p=P)).then_inc(top_in, 16)
            sp.dma_start(top3[:, 0, :], a["top3"]).then_inc(top_in, 16)
            sp.dma_start(bias1[:, 0, :], a["bias1"]).then_inc(top_in, 16)
            sp.dma_start(bias2[:, 0, :], a["bias2"]).then_inc(top_in, 16)
            sp.dma_start(packed[K:K + CTX, 1, :], a["ctxT"]).then_inc(top_in, 16)
            sp.wait_ge(top_copied, len(top_steps))
            sp.dma_start(a["out"].rearrange("b o -> o b"), y[0:1, 0, :]).then_inc(out_done, 16)
            sp.wait_ge(out_done, 16)

        @block.gpsimd
        def _(pool):
            pool.memset(w0_square[:], 0.0).then_inc(w0_cleared, 1)

            def alone():
                pool.sem_inc(pool_passed, 1)

            def gather(b, quarter):
                if quarter == 0:
                    wait(pool, ids_in, (b + 1) * 16)
                    wait(pool, split, b * SPLIT_STEPS)
                    alone()
                for m in range(quarter * M // 4, (quarter + 1) * M // 4):
                    pool.indirect_dma_start(emb[:, m * D:(m + 1) * D], None, a[f"tbl_{m}"],
                                            bass.IndirectOffsetOnAxis(ids[:, m:m + 1], 0)).then_inc(gathered, 16)

            def split_parts(b):
                src = emb[:].rearrange("p (m d) -> p m d", d=D)
                rst = rest[:].rearrange("p (m d) -> p m d", d=D)
                part = [parts[:, :, i, :].rearrange("p d m -> p m d") for i in range(PARTS)]
                wait(pool, gathered, (b + 1) * (16 * M))
                wait(pool, turned_done, b * PAIRS)
                alone()
                pool.tensor_copy(part[0], src).then_inc(split, 1)
                pool.wait_ge(split, b * SPLIT_STEPS + 1)
                pool.tensor_tensor(rst, src, part[0], ALU.subtract).then_inc(split, 1)
                pool.wait_ge(split, b * SPLIT_STEPS + 2)
                alone()
                pool.tensor_copy(part[1], rst).then_inc(split, 1)
                pool.wait_ge(split, b * SPLIT_STEPS + 3)
                pool.tensor_tensor(part[2], rst, part[1], ALU.subtract).then_inc(split, 1)

            def add_up(l, b, j):
                r = relu_out[l]
                pool.wait_ge(relu_ready[l], (b * PAIRS + (j + 1)) * (1 if l == 0 else 2))
                if j == 0:
                    pool.tensor_tensor(zsum_a[:, l], r[:, 0], r[:, 1], ALU.add).then_inc(relu_used[l], 1)
                    return
                pool.tensor_tensor(zsum_b[:], r[:, 0], r[:, 1], ALU.add).then_inc(relu_used[l], 1)
                pool.wait_ge(relu_used[l], b * PAIRS + 2)
                wait(pool, zsum_step[l], b * 2)
                pool.tensor_tensor(zsum_c[:, l], zsum_a[:, l], zsum_b[:], ALU.add).then_inc(zsum_step[l], 1)
                pool.wait_ge(zsum_step[l], b * 2 + 1)
                pool.tensor_tensor(zsum[:, l, bass.ds(b * P, P)], zsum_c[:, l, 0:P], zsum_c[:, l, P:Q],
                                   ALU.add).then_inc(zsum_step[l], 1)

            def body(b, behind_last=False, ahead=2):
                if ahead >= 1:
                    split_parts(b + 1)
                if ahead >= 2:
                    gather(b + 2, 0)
                if behind_last:
                    add_up(2, b - 1, 1)
                add_up(1, b, 0)
                add_up(0, b, 1)
                if ahead >= 2:
                    gather(b + 2, 1)
                    gather(b + 2, 2)
                add_up(2, b, 0)
                if ahead >= 2:
                    gather(b + 2, 3)
                add_up(1, b, 1)
                if ahead >= 1:
                    add_up(0, b + 1, 0)

            for quarter in range(4):
                gather(0, quarter)
            split_parts(0)
            pool.wait_ge(w0_in, 48)
            last = (SHIFTS % GROUP or GROUP) - 1
            pool.tensor_tensor(w0[:, 0:GROUP - 1], w0[:, 0:GROUP - 1], w0_other[:, 0:GROUP - 1], ALU.add).then_inc(w0_summed, 1)
            pool.tensor_tensor(w0[0:M * last, GROUP - 1], w0[0:M * last, GROUP - 1], w0_other[0:M * last, GROUP - 1],
                               ALU.add).then_inc(w0_summed, 1)
            for quarter in range(4):
                gather(1, quarter)
            add_up(0, 0, 0)
            body(0)
            with pool.Fori(1, BLOCKS - 2) as b:
                body(b, behind_last=True)
            body(BLOCKS - 2, behind_last=True, ahead=1)
            body(BLOCKS - 1, behind_last=True, ahead=0)
            add_up(2, BLOCKS - 1, 1)

        @block.tensor
        def _(pe):
            def transposes(b, j):
                pe.wait_ge(split, (b + 1) * SPLIT_STEPS)
                wait(pe, relu_ready[0], b * PAIRS + j)
                for d in range(2 * UNIT_D):
                    mm = pe.transpose(turned[:, d * P:(d + 1) * P],
                                      parts[:, 2 * UNIT_D * j + d].rearrange("p c m -> p (c m)"), ident[:])
                mm.then_inc(turned_done, 1)

            def slot(p, s):
                if s == 0:
                    pe.wait_ge(partsT_ready, p + 1)
                if s < 2 * SLOTS_0:
                    u, which = divmod(s, SLOTS_0)
                else:
                    u, which = divmod(s - 2 * SLOTS_0, TILES)
                    which += SLOTS_0
                wait(pe, slot_copied, p * SLOTS + (s + 1 - RING))
                pe.matmul(ring[s % RING][:], sel[:, which, :], partsT[:, u * UNIT:(u + 1) * UNIT],
                          start=True, stop=True).then_inc(slot_done, 1)

            def products(b, j, group, between=()):
                n, buf, l, u, k = group
                p = b * PAIRS + j
                pe.wait_ge(z_ready, n + 1)
                sums = acc0[:, u] if l == 0 else acc[u][:, 0:Q]
                if l == 1 and k == 0:
                    wait(pe, relu_ready[2], 2 * p + (u - 1))
                if l == 2 and k == 0:
                    pe.wait_ge(xin_ready[u], 2 * p + 2)
                if l == 0:
                    pe.wait_ge(squares_ready, 2 * p + (2 + u + 1))
                    square = x0_square(1 - j, u)
                    for q in range(2):
                        pe.matmul(sums[HALF * q:HALF * (q + 1), :], w0_square[:], square[:, q * Q:(q + 1) * Q],
                                  start=True, stop=False)
                w = (w0, w1, w2)[l]
                ends = l == 0 or k == GROUPS - 1
                for t in range(GROUP):
                    for q in range(2):
                        mm = pe.matmul(sums[HALF * q:HALF * (q + 1), :], w[:, k * GROUP + t, :],
                                       z[:, buf, t, q * Q:(q + 1) * Q],
                                       start=l > 0 and k == 0 and t == 0, stop=ends and t == GROUP - 1)
                    if t == GROUP - 1:
                        mm.then_inc(z_used, 1)
                    for i, s in enumerate(between):
                        if SLOT_BEHIND[i] == t:
                            slot(p + 1, s)

            def top_step(step):
                layer, c, r, needed = top_steps[step]
                cols = ranges[r]
                if step == 0:
                    pe.wait_ge(slot_copied, BLOCKS * PAIRS * SLOTS)
                    pe.wait_ge(top_in, 7 * 16)
                if layer == 1 and c == 0:
                    pe.wait_ge(top_packed, 3 if r < 2 else 6)
                wait(pe, top_copied, max(needed, step + 1 - RING))
                m = P
                if layer == 1:
                    terms = [(top1[0:k, i, c * P:(c + 1) * P], packed[0:k, i, cols]) for i, k in enumerate((P, K + CTX))]
                elif layer == 2:
                    terms = [(top2[:, i, c * P:(c + 1) * P], hid1[:, i, cols]) for i in range(F_TOP1 // P)]
                else:
                    m = 1
                    terms = [(top3[:, 0, i:i + 1], hid2[:, i, cols]) for i in range(F_TOP2 // P)]
                for i, (w, x) in enumerate(terms):
                    mm = pe.matmul(ring[step % RING][0:m, 0:cols.stop - cols.start], w, x,
                                   start=i == 0, stop=i == len(terms) - 1)
                mm.then_inc(top_done, 1)

            def pair(b, j, last=False):
                nb, nj = (b, 1) if j == 0 else (b + 1, 0)
                for g, group in enumerate(groups(b, j, last)):
                    products(b, j, group, () if last else behind(g))
                    if not last and g == TURN_BEHIND:
                        transposes(nb, nj)
                    if last and g >= TOP_BEHIND:
                        top_step(g - TOP_BEHIND)

            pe.wait_ge(const_in, 32)
            transposes(0, 0)
            for s in range(SLOTS):
                slot(0, s)
                if s == FIRST_LAYER0:
                    pe.wait_ge(w0_in, 48)
                    pe.wait_ge(w0_summed, 2)
                    for group in first_groups:
                        products(-1, 1, group)
            pe.wait_ge(w12_in, 32)
            for j in range(PAIRS):
                pair(0, j)
            with pe.Fori(1, BLOCKS - 1) as b:
                for j in range(PAIRS):
                    pair(b, j)
            pair(BLOCKS - 1, 0)
            pair(BLOCKS - 1, 1, last=True)

            for step in range(EARLY, len(top_steps)):
                top_step(step)

        @block.scalar
        def _(act):
            def copy_parts(p):
                act.wait_ge(turned_done, p + 1)
                act.copy(partsT[:], turned[:]).then_inc(partsT_ready, 1)

            def copy_slot(p, par, s, layer0_used):
                if s == LATE_SLOT:
                    act.wait_ge(z_used, layer0_used)
                act.wait_ge(slot_done, p * SLOTS + (s + 1))
                bank = ring[s % RING][:]
                if s < 2 * SLOTS_0:
                    u, which = divmod(s, SLOTS_0)
                    if which == 0:
                        act.activation(x0_square(par, u), bank, ACT.Square).then_inc(squares_ready, 1)
                        out = x0_rep(par, u)
                    else:
                        out = x0_shifts(par, u)[:, which - 1]
                else:
                    u, t = divmod(s - 2 * SLOTS_0, TILES)
                    out = rep[:, par, u, t, :]
                act.copy(out, bank).then_inc(slot_copied, 1)

            def relu(l, u, pairs_before):
                if u == 0:
                    wait(act, relu_used[l], pairs_before)
                out, sums = (relu_out[0][:], acc0[:]) if l == 0 else (relu_out[l][:, u], acc[u][:, 0:Q])
                act.activation(out, sums, ACT.Relu).then_inc(relu_ready[l], 1)

            def next_input(l, u, i):
                q, half = divmod(i, 2)
                sums = relu_out[0][:, u] if l == 0 else acc[u][:, 0:Q]
                ins = act.activation(xin[u][HALF * half:HALF * (half + 1), q * Q:(q + 1) * Q],
                                     sums[HALF * q:HALF * (q + 1)], ACT.Relu)
                if i == 3:
                    ins.then_inc(xin_ready[u], 1)

            def behind_slot(p, s):
                number = lambda g: p * STEP_GROUPS + (2 + g + 1)
                for u in range(2):
                    k = s - first_slot(GROUPS * (u + 1))
                    if k == 0:
                        act.wait_ge(z_used, number(GROUPS * (u + 1) - 1))
                        relu(1, u, p)
                    elif 0 < k <= 4:
                        next_input(1, u, k - 1)
                    k = s - first_slot((12, 16)[u])
                    if k == 0:
                        act.wait_ge(z_ready, number((13, 17)[u]))
                        act.wait_ge(relu_ready[0], p + 2)
                    if 0 <= k < 4:
                        next_input(0, u, k)
                if s == first_slot(10):
                    act.wait_ge(z_used, number(9))
                    relu(0, 0, p + 1)
                if s == first_slot(14):
                    act.wait_ge(z_used, number(13))
                    relu(2, 0, p)

            def shift_sums(cols, steps):
                for l, (to, of) in enumerate(((0, 1), (1, 0), (0, 1))):
                    act.wait_ge(zsum_step[l], steps)
                    act.copy(shifted[HALF * to:HALF * (to + 1), l, cols],
                             zsum[HALF * of:HALF * (of + 1), l, cols]).then_inc(top_shifted, 1)

            def top_copy(step):
                layer, c, r, _ = top_steps[step]
                cols = ranges[r]
                if step == 0:
                    act.wait_ge(top_in, 7 * 16)
                act.wait_ge(top_done, step + 1)
                bank = ring[step % RING][0:1 if layer == 3 else P, 0:cols.stop - cols.start]
                if layer == 1:
                    ins = act.activation(hid1[:, c, cols], bank, ACT.Relu, bias=bias1[:, 0, c:c + 1])
                elif layer == 2:
                    ins = act.activation(hid2[:, c, cols], bank, ACT.Relu, bias=bias2[:, 0, c:c + 1])
                else:
                    ins = act.copy(y[0:1, 0, cols], bank)
                ins.then_inc(top_copied, 1)

            def pair(b, j, first=False, last=False):
                p = b * PAIRS + j
                if not first:
                    act.wait_ge(z_used, p * STEP_GROUPS + 2)
                    relu(2, 1, p)
                if not last:
                    copy_parts(p + 1)
                    for s in range(SLOTS):
                        copy_slot(p + 1, 1 - j, s, p * STEP_GROUPS + (2 + 9 + 1))
                        behind_slot(p, s)
                    return
                shift_sums(slice(0, last_rows), 2 * (BLOCKS - 1))
                for g, (n, _, l, u, k) in enumerate(groups(b, j, last)):
                    if k == GROUPS - 1:
                        act.wait_ge(z_used, n + 1)
                        relu(l, u, p)
                        if l == 1:
                            for i in range(4):
                                next_input(1, u, i)
                    if g >= TOP_BEHIND:
                        top_copy(g - TOP_BEHIND)

            copy_parts(0)
            for s in range(SLOTS):
                copy_slot(0, 0, s, 2)
                if s == FIRST_LAYER0:
                    act.wait_ge(z_used, 2)
                    relu(0, 0, 0)
                    act.wait_ge(relu_ready[0], 1)
                    for u in range(2):
                        for i in range(4):
                            next_input(0, u, i)
            pair(0, 0, first=True)
            pair(0, 1)
            with act.Fori(1, BLOCKS - 1) as b:
                for j in range(PAIRS):
                    pair(b, j)
            pair(BLOCKS - 1, 0)
            pair(BLOCKS - 1, 1, last=True)

            shift_sums(slice(last_rows, ROWS), 2 * BLOCKS)
            for step in range(EARLY, len(top_steps)):
                top_copy(step)

        @block.vector
        def _(dve):
            def multiply(b, j, group):
                n, buf, l, u, k = group
                p = b * PAIRS + j
                wait(dve, z_used, n - (Z_BUFS - 1))
                if l == 0:
                    dve.wait_ge(slot_copied, (p + 1) * SLOTS + SLOTS_0 * (u + 1))
                    tiles, other = x0_shifts(1 - j, u), x0_rep(1 - j, u)
                else:
                    if k == 0:
                        dve.wait_ge(xin_ready[u], 2 * p + l)
                    if l == 1:
                        dve.wait_ge(slot_copied, p * SLOTS + (2 * SLOTS_0 + TILES * u + GROUP * (k + 1)))
                    tiles, other = rep[:, j, u, GROUP * k:GROUP * (k + 1), :], xin[u][:]
                dve.tensor_tensor(z[:, buf], tiles, other.unsqueeze(1).to_broadcast([P, GROUP, UNIT]),
                                  ALU.mult).then_inc(z_ready, 1)

            for group in first_groups:
                multiply(-1, 1, group)
            for j in range(PAIRS):
                for group in groups(0, j):
                    multiply(0, j, group)
            with dve.Fori(1, BLOCKS - 1) as b:
                for j in range(PAIRS):
                    for group in groups(b, j):
                        multiply(b, j, group)
            def pack(cols, before):
                for l, (h, c) in enumerate(((0, 0), (1, 0), (0, 1))):
                    dve.wait_ge(top_shifted, before + l + 1)
                    rows = slice(HALF * h, HALF * (h + 1))
                    dve.tensor_tensor(packed[rows, c, cols], zsum[rows, l, cols], shifted[rows, l, cols],
                                      ALU.add).then_inc(top_packed, 1)

            for j in range(PAIRS):
                for g, group in enumerate(groups(BLOCKS - 1, j, j == PAIRS - 1)):
                    if j == PAIRS - 1 and g == Z_BUFS:
                        pack(slice(0, last_rows), 0)
                    multiply(BLOCKS - 1, j, group)
            pack(slice(last_rows, ROWS), 3)


def kernel(**inputs):
    import concourse.bacc as bacc
    from concourse.bass_utils import run_bass_kernel_spmd

    w0 = inputs["L0_rec_W0"]
    m = np.arange(M)
    shift = np.arange(1, SHIFTS + 1)[:, None]
    arrays = {
        "ids": inputs["ids"],
        "selections": selections(),
        "identity": identity(),
        "w0_mh": w0[m, (m + shift) % M].reshape(SHIFTS * M, K),
        "w0_hm": w0[(m + shift) % M, m].reshape(SHIFTS * M, K),
        "w0_mm": w0[m, m],
        "L0_rec_W1": inputs["L0_rec_W1"],
        "L0_rec_W2": inputs["L0_rec_W2"],
        "W_top1": inputs["W_top1"],
        "W_top2": inputs["W_top2"],
        "top3": inputs["W_top3"].reshape(F_TOP2 // P, P).T,
        "bias1": inputs["b_top1"].reshape(F_TOP1 // P, P).T,
        "bias2": inputs["b_top2"].reshape(F_TOP2 // P, P).T,
        "ctxT": inputs["dense_ctx"].T,
    }
    arrays.update({f"tbl_{i}": inputs[f"tbl_{i}"] for i in range(M)})
    arrays = {name: np.ascontiguousarray(x) for name, x in arrays.items()}

    nc = bacc.Bacc("TRN2", target_bir_lowering=False, num_devices=1)
    aps = {name: nc.dram_tensor("in_" + name, x.shape, mybir.dt.from_np(x.dtype), kind="ExternalInput").ap()
           for name, x in arrays.items()}
    aps["out"] = nc.dram_tensor("out", (ROWS, 1), F32, kind="ExternalOutput").ap()
    build(nc, aps)
    result = run_bass_kernel_spmd(nc, [{"in_" + name: x for name, x in arrays.items()}], core_ids=[0])
    return result.results[0]["out"]
```

```python
from contextlib import ExitStack

import numpy as np

import concourse.bass as bass
from concourse import mybir

F32 = mybir.dt.float32
BF16 = mybir.dt.bfloat16
I32 = mybir.dt.int32
ALU = mybir.AluOpType
ACT = mybir.ActivationFunctionType

P = 128
HALF = 64
ROWS = 1024
M = 32
D = 16
K = 64
PARTS = 3
CTX = 16
BLOCKS = ROWS // P
UNITS = 2
UNIT_D = 4
UNIT = UNIT_D * P
COLS = UNITS * UNIT
Q = UNIT // 2
HALVES = 2
STEPS = BLOCKS * HALVES
QUAD = 32
QUADS = P // QUAD
ORDERS = K // QUAD
TILES = M // QUADS
GROUP = 2
PER_ORDER = TILES // GROUP
GROUPS = ORDERS * PER_ORDER
PRODUCTS = 2 * GROUPS
READY = PRODUCTS + 1
LAYER0_SHIFTS = ((0, 0, 0, 0), (6, 9, 13, 16), (1, 8, 12, 4), (3, 19, 27, 9))
LAYER0_PAIRS = ((0, 1), (0, 2), (3, 1), (3, 2))
SHIFT_16 = 3 * QUAD
Z_BUFS = 4
RING = 2
SLOTS_0 = UNITS * len(LAYER0_SHIFTS)
SLOTS = SLOTS_0 + UNITS * TILES
TURN_BEHIND = 0
FIRST_LAYER0 = SLOTS_0 + 3
FIRST = M - 4
WARM = 20
WARM_TURN, WARM_END = 5, 14
SPLIT_STEPS = 4
F_TOP1, F_TOP2 = 512, 256


def selections():
    one = np.uint16(0x3F80)
    sel = np.zeros((PARTS, M, len(LAYER0_SHIFTS) + TILES, P), np.uint16)
    for p in range(P):
        for i, shifts in enumerate(LAYER0_SHIFTS):
            sel[:, (p + shifts[p // QUAD]) % M, i, p] = one
        for t in range(TILES):
            sel[:, QUADS * t + p // QUAD, len(LAYER0_SHIFTS) + t, p] = one
    return sel.reshape(PARTS * M, -1)


def identity():
    return (np.eye(P) * 0x3F80).astype(np.uint16)


def by_orders(w):
    p = np.arange(P)
    quad = p // QUAD
    o, t = np.arange(ORDERS)[:, None, None], np.arange(TILES)[None, :, None]
    m = QUADS * t + quad + 0 * o
    h = QUAD * ((quad + o) % ORDERS) + p % QUAD + 0 * t
    return w[m, h].reshape(ORDERS * TILES, P, K)


def layer0_rows():
    p = np.arange(P)
    shifts = np.array(LAYER0_SHIFTS)[:, p // QUAD]
    m, h = ((p + shifts[[pair[i] for pair in LAYER0_PAIRS]]) % M for i in range(2))
    difference = (m - h) % M
    assert set(np.minimum(difference, M - difference).ravel()) == set(range(1, M // 2 + 1))
    return m.ravel(), h.ravel()


def slot_plan():
    return [0, 0, 2, 2, 2, 2, 2, 0] + [1, 2] + [1, 2, 1, 2, 1, 2, 1, 1]


def build(nc, a):
    plan = slot_plan()
    assert sum(plan) == SLOTS

    with ExitStack() as ctx:
        def sb(name, shape, dt):
            return ctx.enter_context(nc.sbuf_tensor(name, shape, dt))

        def psum(name, shape, dt):
            return ctx.enter_context(nc.psum_tensor(name, shape, dt))

        def sem(name):
            return ctx.enter_context(nc.semaphore(name))

        rep = sb("rep", [P, 2, TILES, COLS], F32)
        z = sb("z", [P, Z_BUFS, GROUP, COLS], F32)
        x0_rep = sb("x0_rep", [P, len(LAYER0_SHIFTS), COLS], F32)
        x0_square = sb("x0_square", [P, COLS], F32)
        z0 = sb("z0", [P, 2 * GROUP, COLS], F32)
        w1 = sb("w1", [P, ORDERS * TILES, K], F32)
        w2 = sb("w2", [P, ORDERS * TILES, K], F32)
        w0 = sb("w0", [P, 2 * GROUP, K], F32)
        w0_other = sb("w0_other", [P, 2 * GROUP, K], F32)
        w0_square = sb("w0_square", [P, K], F32)
        sel = sb("sel", [PARTS * M, len(LAYER0_SHIFTS) + TILES, P], BF16)
        ident = sb("ident", [P, P], BF16)
        ids = sb("ids", [P, M], I32)
        emb = sb("emb", [P, M * D], F32)
        rest = sb("rest", [P, M * D], F32)
        parts = sb("parts", [P, D, PARTS, M], BF16)
        partsT = sb("partsT", [PARTS * M, COLS], BF16)
        relu_out = [sb(f"relu_out{l}", [P, UNIT], F32) for l in range(3)]
        zsum_a = sb("zsum_a", [P, 3, Q], F32)
        zsum_b = sb("zsum_b", [P, Q], F32)
        zsum_c = sb("zsum_c", [P, 3, Q], F32)
        zsum = sb("zsum", [P, 3, ROWS], F32)
        shifted = sb("shifted", [P, 3, ROWS], F32)
        y = sb("y", [1, ROWS], F32)

        xin = [psum(f"xin{o}", [P, COLS], F32) for o in range(ORDERS)]
        acc = [psum(f"acc{par}", [P, UNIT], F32) for par in range(2)]
        ring = [psum(f"ring{r}", [P, UNIT], F32) for r in range(RING)]

        const_in = sem("const_in")
        w0_cleared, w0_in, w0_summed = sem("w0_cleared"), sem("w0_in"), sem("w0_summed")
        w12_in = sem("w12_in")
        ids_in, gathered, split = sem("ids_in"), sem("gathered"), sem("split")
        pool_passed = sem("pool_passed")
        gathered_first = sem("gathered_first")
        turned_done, partsT_ready = sem("turned_done"), sem("partsT_ready")
        slot_done, slot_copied, squares_ready = sem("slot_done"), sem("slot_copied"), sem("squares_ready")
        z_ready, z_used = sem("z_ready"), sem("z_used")
        z0_half_ready, z0_used = [sem(f"z0_half{i}_ready") for i in range(2)], sem("z0_used")
        xin_ready = [sem(f"xin{o}_ready") for o in range(ORDERS)]
        relu_ready = [sem(f"relu{l}_ready") for l in range(3)]
        relu_used = [sem(f"relu{l}_used") for l in range(3)]
        zsum_step = [sem(f"zsum{l}_step") for l in range(3)]
        top_in, top_shifted = sem("top_in"), sem("top_shifted")
        top_packed, last_packed, last_added = sem("top_packed"), sem("last_packed"), sem("last_added")
        top_done, top_copied, out_done = sem("top_done"), sem("top_copied"), sem("out_done")

        def wait(eng, s, value):
            if not isinstance(value, int) or value > 0:
                eng.wait_ge(s, value)

        layers_12 = [(l, k) for l in (1, 2) for k in range(GROUPS)]
        works = layers_12[:GROUPS] + [(0, 0), (0, 1)] + layers_12[GROUPS:]

        def used(p, l, k):
            return p * PRODUCTS + ((l - 1) * GROUPS + k + 1)

        def ready(p, l, k, tile=GROUP - 1):
            split_before = 1 if (l, k) > (1, GROUPS - 1) or (l, k, tile) == (1, GROUPS - 1, GROUP - 1) else 0
            return p * READY + ((l - 1) * GROUPS + k + 1 + split_before)

        def ring_bank(par, item):
            return ring[(par + item) % RING]

        def turned(par):
            return ring_bank(par, 0)[0:PARTS * M].bitcast(BF16)

        def pack(eng, cols, before, packed_sem, one_by_one=False):
            for l, (h, c) in enumerate(((0, 0), (1, 0), (0, 1))):
                eng.wait_ge(top_shifted, before + l + 1)
                rows = slice(HALF * h, HALF * (h + 1))
                eng.tensor_tensor(packed[rows, c, cols], zsum[rows, l, cols], shifted[rows, l, cols],
                                  ALU.add).then_inc(packed_sem, 1)
                if one_by_one:
                    eng.wait_ge(packed_sem, l + 1)

        def exact_split(eng, b, alone):
            src = emb[:].rearrange("p (m d) -> p m d", d=D)
            rst = rest[:].rearrange("p (m d) -> p m d", d=D)
            part = [parts[:, :, i, :].rearrange("p d m -> p m d") for i in range(PARTS)]
            eng.tensor_copy(part[0], src).then_inc(split, 1)
            eng.wait_ge(split, b * SPLIT_STEPS + 1)
            eng.tensor_tensor(rst, src, part[0], ALU.subtract).then_inc(split, 1)
            eng.wait_ge(split, b * SPLIT_STEPS + 2)
            alone()
            eng.tensor_copy(part[1], rst).then_inc(split, 1)
            eng.wait_ge(split, b * SPLIT_STEPS + 3)
            eng.tensor_tensor(part[2], rst, part[1], ALU.subtract).then_inc(split, 1)

        def layer0_operands(i):
            return (z0[:, GROUP * i:GROUP * (i + 1)],
                    x0_rep[:, 3 * i].unsqueeze(1).to_broadcast([P, GROUP, COLS]), x0_rep[:, 1:3])

        layer0_slots = (3 * UNITS, 4 * UNITS)

        def first_slot(g):
            return sum(plan[:g])

        def behind(g):
            return range(first_slot(g), first_slot(g + 1))

        def spare(buffer, *shapes):
            flat, at, pieces = buffer, 0, []
            for c, n in shapes:
                pieces.append(flat[:, at:at + c * n].rearrange("p (c n) -> p c n", c=c))
                at += c * n
            return pieces

        hid1, hid2 = spare(rep[:, 0].rearrange("p t n -> p (t n)"), (F_TOP1 // P, ROWS), (F_TOP2 // P, ROWS))
        packed, top1, top2 = spare(x0_rep[:].rearrange("p t n -> p (t n)"),
                                   (2, ROWS), (2, F_TOP1), (F_TOP1 // P, F_TOP2))
        top3, bias1, bias2 = spare(z0[:].rearrange("p t n -> p (t n)"),
                                   (1, F_TOP2 // P), (1, F_TOP1 // P), (1, F_TOP2 // P))

        last_rows = ROWS - P
        ranges = [slice(0, 512), slice(512, last_rows), slice(last_rows, ROWS)]
        tiles = {1: F_TOP1 // P, 2: F_TOP2 // P, 3: 1}
        top_steps = []
        for together in ((0, 1), (2,)):
            for layer in (1, 2, 3):
                for r in together:
                    needed = [n + 1 for n, x in enumerate(top_steps) if x[0] == layer - 1 and x[2] == r]
                    top_steps += [(layer, c, r, max(needed, default=0)) for c in range(tiles[layer])]
        EARLY = len(top_steps) - sum(tiles.values())

        def top_bank(step):
            if step < EARLY:
                return ring[step % RING]
            return (ring[0], acc[0], xin[0][:, 0:UNIT], xin[0][:, UNIT:COLS], xin[1][:, 0:UNIT],
                    xin[1][:, UNIT:COLS], ring[1])[step - EARLY]

        top_plan = [0] + [1] * 6 + [3] + [1] * 5 + [0] * 3
        assert sum(top_plan) == EARLY

        def top_behind(i):
            return range(sum(top_plan[:i]), sum(top_plan[:i + 1]))

        block = ctx.enter_context(nc.Block())

        @block.sync
        def _(sp):
            sp.dma_start(ids[:], a["ids"][0:P, :]).then_inc(ids_in, 16)
            sp.dma_start(ident[:], a["identity"].bitcast(BF16)).then_inc(const_in, 16)
            sp.dma_start(sel[:], a["selections"].bitcast(BF16).rearrange("k (s p) -> k s p", p=P)
                         ).then_inc(const_in, 16)
            sp.dma_start(w0[:], a["w0_mh"].rearrange("(j p) k -> p j k", p=P)).then_inc(w0_in, 16)
            sp.dma_start(w0_other[:], a["w0_hm"].rearrange("(j p) k -> p j k", p=P)).then_inc(w0_in, 16)
            sp.wait_ge(w0_cleared, 1)
            sp.dma_start(w0_square[0:M, :], a["w0_mm"]).then_inc(w0_in, 16)
            sp.dma_start(w1[:], a["w1"].rearrange("t p k -> p t k")).then_inc(w12_in, 16)
            sp.dma_start(w2[:], a["w2"].rearrange("t p k -> p t k")).then_inc(w12_in, 16)
            sp.wait_ge(gathered_first, 16 * FIRST)
            with sp.Fori(1, BLOCKS) as b:
                sp.wait_ge(gathered, b * (16 * M) - 16 * FIRST)
                sp.dma_start(ids[:], a["ids"][bass.ds(b * P, P), :]).then_inc(ids_in, 16)
            sp.wait_ge(z0_used, STEPS)
            sp.dma_start(top1[:, 0, :], a["W_top1"][0:P, :]).then_inc(top_in, 16)
            sp.dma_start(top1[0:K + CTX, 1, :], a["W_top1"][P:3 * K + CTX, :]).then_inc(top_in, 16)
            sp.dma_start(top2, a["W_top2"].rearrange("(c p) n -> p c n", p=P)).then_inc(top_in, 16)
            sp.dma_start(top3[:, 0, :], a["top3"]).then_inc(top_in, 16)
            sp.dma_start(bias1[:, 0, :], a["bias1"]).then_inc(top_in, 16)
            sp.dma_start(bias2[:, 0, :], a["bias2"]).then_inc(top_in, 16)
            sp.dma_start(packed[K:K + CTX, 1, :], a["ctxT"]).then_inc(top_in, 16)
            sp.wait_ge(top_copied, len(top_steps))
            sp.dma_start(a["out"].rearrange("b o -> o b"), y[:]).then_inc(out_done, 16)
            sp.wait_ge(out_done, 16)

        @block.gpsimd
        def _(pool):
            pool.memset(w0_square[:], 0.0).then_inc(w0_cleared, 1)

            def alone():
                pool.sem_inc(pool_passed, 1)

            def gather(b, quarter):
                if quarter == 0:
                    wait(pool, ids_in, (b + 1) * 16)
                    wait(pool, split, b * SPLIT_STEPS)
                    alone()
                first_block = isinstance(b, int) and b == 0
                for m in range(quarter * M // 4, (quarter + 1) * M // 4):
                    done = gathered_first if first_block and m < FIRST else gathered
                    pool.indirect_dma_start(emb[:, m * D:(m + 1) * D], None, a[f"tbl_{m}"],
                                            bass.IndirectOffsetOnAxis(ids[:, m:m + 1], 0)).then_inc(done, 16)

            def split_parts(b):
                pool.wait_ge(gathered, b * (16 * M) + 16 * (M - FIRST))
                pool.wait_ge(turned_done, b * HALVES)
                alone()
                exact_split(pool, b, alone)

            def multiply0(b, j):
                p = b * HALVES + j
                pool.wait_ge(slot_copied, p * SLOTS + layer0_slots[0])
                pool.wait_ge(z0_used, p)
                pool.tensor_tensor(*layer0_operands(0), ALU.mult).then_inc(z0_half_ready[0], 1)

            def add_up(l, b, j):
                r = relu_out[l][:].rearrange("p (i n) -> p i n", i=2)
                pool.wait_ge(relu_ready[l], b * HALVES + (j + 1))
                if j == 0:
                    pool.tensor_tensor(zsum_a[:, l], r[:, 0], r[:, 1], ALU.add).then_inc(relu_used[l], 1)
                    return
                pool.tensor_tensor(zsum_b[:], r[:, 0], r[:, 1], ALU.add).then_inc(relu_used[l], 1)
                pool.wait_ge(relu_used[l], b * HALVES + 2)
                wait(pool, zsum_step[l], b * 2)
                pool.tensor_tensor(zsum_c[:, l], zsum_a[:, l], zsum_b[:], ALU.add).then_inc(zsum_step[l], 1)
                pool.wait_ge(zsum_step[l], b * 2 + 1)
                pool.tensor_tensor(zsum[:, l, bass.ds(b * P, P)], zsum_c[:, l, 0:P], zsum_c[:, l, P:Q],
                                   ALU.add).then_inc(zsum_step[l], 1)

            def body(b, ahead=2, first=False):
                if ahead >= 1:
                    gather(b + 1, 3)
                add_up(0, b, 0)
                if first:
                    multiply0(b, 1)
                if ahead >= 1:
                    split_parts(b + 1)
                if not first:
                    multiply0(b, 1)
                    add_up(2, b - 1, 1)
                if ahead == 0:
                    pool.wait_ge(z0_used, STEPS)
                    pool.wait_ge(zsum_step[2], 2 * (BLOCKS - 1))
                    pack(pool, slice(0, last_rows), 0, top_packed, one_by_one=True)
                if ahead >= 2:
                    gather(b + 2, 0)
                add_up(1, b, 0)

                if ahead >= 2:
                    gather(b + 2, 1)
                add_up(2, b, 0)
                add_up(0, b, 1)
                if ahead >= 1:
                    multiply0(b + 1, 0)
                if ahead >= 2:
                    gather(b + 2, 2)
                add_up(1, b, 1)

            for quarter in range(4):
                gather(0, quarter)
            for quarter in range(3):
                gather(1, quarter)
            body(0, first=True)
            with pool.Fori(1, BLOCKS - 2) as b:
                body(b)
            body(BLOCKS - 2, ahead=1)
            body(BLOCKS - 1, ahead=0)

        @block.tensor
        def _(pe):
            def transposes(b, j):
                pe.wait_ge(split, (b + 1) * SPLIT_STEPS)
                wait(pe, slot_copied, (b * HALVES + j) * SLOTS - 1)
                for d in range(2 * UNIT_D):
                    mm = pe.transpose(turned(j)[:, d * P:(d + 1) * P],
                                      parts[:, 2 * UNIT_D * j + d].rearrange("p c m -> p (c m)"), ident[:])
                mm.then_inc(turned_done, 1)

            def slot(b, j, s):
                p = b * HALVES + j
                if s == 0:
                    pe.wait_ge(partsT_ready, p + 1)
                if s != 1:
                    wait(pe, slot_copied, p * SLOTS + (s - 1) if s else p * SLOTS)
                which, u = divmod(s, UNITS)
                pe.matmul(ring_bank(j, 1 + s)[:], sel[:, which, :], partsT[:, u * UNIT:(u + 1) * UNIT],
                          start=True, stop=True).then_inc(slot_done, 1)

            def run_tiles(sums, w, z_tiles, start, stop, last_inc, between, nb, nj, next_tile_ready=None):
                for t in range(GROUP):
                    if t and next_tile_ready is not None:
                        pe.wait_ge(z_ready, next_tile_ready)
                    for u in range(UNITS):
                        mm = pe.matmul(sums[HALF * u:HALF * (u + 1), :], w[:, t, :],
                                       z_tiles[:, t, u * UNIT:(u + 1) * UNIT],
                                       start=start and t == 0, stop=stop and t == GROUP - 1)
                    if t == GROUP - 1 and last_inc is not None:
                        mm.then_inc(last_inc, 1)
                    for s in list(between)[t:t + 1]:
                        slot(nb, nj, s)

            def products(b, j, l, k, nb, nj, between=()):
                p = b * HALVES + j
                n = layers_12.index((l, k))
                pe.wait_ge(z_ready, ready(p, l, k, 0))
                if k == 0:
                    pe.wait_ge(relu_ready[l - 1], p + 1)
                run_tiles(acc[j], (w1, w2)[l - 1][:, k * GROUP:(k + 1) * GROUP, :], z[:, n % Z_BUFS],
                          k == 0, k == GROUPS - 1, z_used, between, nb, nj,
                          ready(p, l, k) if (l, k) == (1, GROUPS - 1) else None)

            def products0(b, j, i, between=()):
                p = b * HALVES + j
                if i == 0:
                    pe.wait_ge(squares_ready, UNITS * (p + 1))
                    if not (isinstance(p, int) and p < 2):
                        pe.wait_ge(relu_ready[2], p - 1)
                    for u in range(UNITS):
                        pe.matmul(acc[j][HALF * u:HALF * (u + 1), :], w0_square[:],
                                  x0_square[:, u * UNIT:(u + 1) * UNIT], start=True, stop=False)
                pe.wait_ge(z0_half_ready[i], p + 1)
                run_tiles(acc[j], w0[:, GROUP * i:GROUP * (i + 1), :], z0[:, GROUP * i:GROUP * (i + 1)],
                          False, i == 1, z0_used if i == 1 else None, between, b, j)

            def top_step(step):
                layer, c, r, needed = top_steps[step]
                cols = ranges[r]
                if step == 0:
                    pe.wait_ge(slot_copied, STEPS * SLOTS)
                    pe.wait_ge(top_in, 7 * 16)
                if layer == 1 and c == 0:
                    pe.wait_ge(top_packed if r < 2 else last_packed, 3)
                wait(pe, top_copied, max(needed, step + 1 - RING if step < EARLY else EARLY))
                m = P
                if layer == 1:
                    terms = [(top1[0:k, i, c * P:(c + 1) * P], packed[0:k, i, cols])
                             for i, k in enumerate((P, K + CTX))]
                elif layer == 2:
                    terms = [(top2[:, i, c * P:(c + 1) * P], hid1[:, i, cols]) for i in range(F_TOP1 // P)]
                else:
                    m = 1
                    terms = [(top3[:, 0, i:i + 1], hid2[:, i, cols]) for i in range(F_TOP2 // P)]
                for i, (w, x) in enumerate(terms):
                    mm = pe.matmul(top_bank(step)[0:m, 0:cols.stop - cols.start], w, x,
                                   start=i == 0, stop=i == len(terms) - 1)
                mm.then_inc(top_done, 1)

            def step_works(b, j):
                nb, nj = (b, 1) if j == 0 else (b + 1, 0)
                for i, (l, k) in enumerate(works):
                    if l == 0:
                        products0(nb, nj, k, behind(i))
                    else:
                        products(b, j, l, k, nb, nj, behind(i))
                    if i == TURN_BEHIND:
                        transposes(nb, nj)

            def keep_warm(n, bank=xin[1][:, 0:UNIT]):
                for _ in range(n):
                    pe.matmul(bank, ident[0:PARTS * M, :], sel[:, 0:4, :].rearrange("k s p -> k (s p)"),
                              start=True, stop=True)

            pe.wait_ge(const_in, 32)
            pe.wait_ge(gathered_first, FIRST * 16)
            keep_warm(WARM)
            transposes(0, 0)
            keep_warm(WARM_TURN)
            for s in range(SLOTS):
                slot(0, 0, s)
                if s < FIRST_LAYER0:
                    keep_warm(1)
                if s == FIRST_LAYER0:
                    pe.wait_ge(w0_in, 48)
                    pe.wait_ge(w0_summed, 2)
                    for i in range(2):
                        products0(0, 0, i)
            pe.wait_ge(w12_in, 32)
            for j in range(HALVES):
                step_works(0, j)
            with pe.Fori(1, BLOCKS - 1) as b:
                for j in range(HALVES):
                    step_works(b, j)
            step_works(BLOCKS - 1, 0)
            for i, (l, k) in enumerate(layers_12):
                products(BLOCKS - 1, 1, l, k, 0, 0)
                for step in top_behind(i):
                    top_step(step)

            pe.wait_ge(top_copied, EARLY)
            keep_warm(WARM_END, ring[1][:])
            for step in range(EARLY, len(top_steps)):
                top_step(step)

        @block.scalar
        def _(act):
            def copy_parts(p, par):
                act.wait_ge(turned_done, p + 1)
                act.copy(partsT[:], turned(par)).then_inc(partsT_ready, 1)

            def copy_slot(p, par, s):
                if s == 0:
                    wait(act, z0_used, p)
                act.wait_ge(slot_done, p * SLOTS + (s + 1))
                bank = ring_bank(par, 1 + s)[:]
                which, u = divmod(s, UNITS)
                cols = slice(u * UNIT, (u + 1) * UNIT)
                if which == 0:
                    act.activation(x0_square[:, cols], bank, ACT.Square).then_inc(squares_ready, 1)
                if s < SLOTS_0:
                    out = x0_rep[:, which, cols]
                else:
                    out = rep[:, par, which - len(LAYER0_SHIFTS), cols]
                act.copy(out, bank).then_inc(slot_copied, 1)

            def relu(l, p, par):
                wait(act, relu_used[l], p)
                act.activation(relu_out[l][:], acc[par][:], ACT.Relu).then_inc(relu_ready[l], 1)

            def natural_order(src, i, func):
                u, half = divmod(i, 2)
                ins = act.activation(xin[0][HALF * half:HALF * (half + 1), u * UNIT:(u + 1) * UNIT],
                                     src[HALF * u:HALF * (u + 1), :], func)
                if half == 1:
                    ins.then_inc(xin_ready[0], 1)

            def swapped_order(l, i):
                u, half, s = i // 4, i // 2 % 2, i % 2
                to, of = HALF * half + QUAD * s, HALF * u + QUAD * (1 - s)
                ins = act.activation(xin[1][to:to + QUAD, u * UNIT:(u + 1) * UNIT], relu_out[l][of:of + QUAD, :],
                                     ACT.Copy)
                if i == 7:
                    ins.then_inc(xin_ready[1], 1)

            def behind_slot(p, j, s):
                k = s - (first_slot(GROUPS) - 1)
                if k == 0:
                    act.wait_ge(z_used, used(p, 1, GROUPS - 1))
                    for i in range(4):
                        natural_order(acc[j], i, ACT.Relu)
                    relu(1, p, j)
                    act.wait_ge(relu_ready[1], p + 1)
                if 0 <= k < 4:
                    for i in (2 * k, 2 * k + 1):
                        swapped_order(1, i)
                if k == 4:
                    act.wait_ge(z0_used, p + 2)
                    relu(0, p + 1, 1 - j)
                    act.wait_ge(relu_ready[0], p + 2)
                k = s - first_slot(GROUPS + 2 + PER_ORDER - 1)
                if k == 0:
                    act.wait_ge(z_ready, ready(p, 2, PER_ORDER - 1))
                if 0 <= k < 2:
                    for i in (2 * k, 2 * k + 1):
                        natural_order(relu_out[0], i, ACT.Copy)

            def shift_sums(l, cols):
                to, of = ((0, 1), (1, 0), (0, 1))[l]
                act.copy(shifted[HALF * to:HALF * (to + 1), l, cols],
                         zsum[HALF * of:HALF * (of + 1), l, cols]).then_inc(top_shifted, 1)

            def top_copy(step):
                layer, c, r, _ = top_steps[step]
                cols = ranges[r]
                if step == 0:
                    act.wait_ge(top_in, 7 * 16)
                act.wait_ge(top_done, step + 1)
                bank = top_bank(step)[0:1 if layer == 3 else P, 0:cols.stop - cols.start]
                if layer == 1:
                    ins = act.activation(hid1[:, c, cols], bank, ACT.Relu, bias=bias1[:, 0, c:c + 1])
                elif layer == 2:
                    ins = act.activation(hid2[:, c, cols], bank, ACT.Relu, bias=bias2[:, 0, c:c + 1])
                else:
                    ins = act.copy(y[:, cols], bank)
                ins.then_inc(top_copied, 1)

            def begin(p):
                if not isinstance(p, int) or p > 0:
                    act.wait_ge(z_ready, p * READY)
                for i in range(8):
                    swapped_order(0, i)

            def relu_before(p, j):
                act.wait_ge(z_used, p * PRODUCTS)
                relu(2, p - 1, 1 - j)

            def step_works(b, j, first=False, last=False):
                p = b * HALVES + j
                begin(p)
                copy_parts(p + 1, 1 - j)
                if not first:
                    relu_before(p, j)
                for s in range(SLOTS):
                    copy_slot(p + 1, 1 - j, s)
                    behind_slot(p, j, s)
                    l = s - (SLOTS - 3)
                    if last and l >= 0:
                        act.wait_ge(zsum_step[l], 2 * (BLOCKS - 1))
                        shift_sums(l, slice(0, last_rows))

            copy_parts(0, 0)
            for s in range(SLOTS):
                copy_slot(0, 0, s)
                if s == FIRST_LAYER0:
                    act.wait_ge(z0_used, 1)
                    relu(0, 0, 0)
                    for i in range(4):
                        natural_order(acc[0], i, ACT.Relu)
                    act.wait_ge(relu_ready[0], 1)
            for j in range(HALVES):
                step_works(0, j, first=j == 0)
            with act.Fori(1, BLOCKS - 1) as b:
                for j in range(HALVES):
                    step_works(b, j)
            step_works(BLOCKS - 1, 0, last=True)

            p = STEPS - 1
            begin(p)
            relu_before(p, 1)
            for i, (l, k) in enumerate(layers_12):
                if k == GROUPS - 1:
                    act.wait_ge(z_used, used(p, l, k))
                    if l == 1:
                        for piece in range(4):
                            natural_order(acc[1], piece, ACT.Relu)
                    relu(l, p, 1)
                for step in top_behind(i):
                    top_copy(step)
                if (l, k) == (1, GROUPS - 1):
                    act.wait_ge(relu_ready[1], p + 1)
                    for piece in range(8):
                        swapped_order(1, piece)

            for l in range(3):
                act.wait_ge(*((zsum_step[l], 2 * BLOCKS) if l < 2 else (last_added, 3)))
                shift_sums(l, slice(last_rows, ROWS))
            for step in range(EARLY, len(top_steps)):
                top_copy(step)

        @block.vector
        def _(dve):
            dve.wait_ge(w0_in, 48)
            dve.tensor_tensor(w0[:, 1:], w0[:, 1:], w0_other[:, 1:], ALU.add).then_inc(w0_summed, 1)
            dve.tensor_tensor(w0[0:SHIFT_16, 0], w0[0:SHIFT_16, 0], w0_other[0:SHIFT_16, 0],
                              ALU.add).then_inc(w0_summed, 1)
            dve.wait_ge(gathered_first, 16 * FIRST)
            dve.wait_ge(gathered, 16 * (M - FIRST))
            exact_split(dve, 0, lambda: None)
            for i in range(2):
                dve.wait_ge(slot_copied, layer0_slots[i])
                dve.tensor_tensor(*layer0_operands(i), ALU.mult).then_inc(z0_half_ready[i], 1)

            def multiply(b, j, l, k):
                p = b * HALVES + j
                n = layers_12.index((l, k))
                order, tile = k // PER_ORDER, k % PER_ORDER * GROUP
                wait(dve, z_used, p * PRODUCTS + (n - (Z_BUFS - 1)))
                if l == 1 and order == 0:
                    dve.wait_ge(slot_copied, p * SLOTS + (SLOTS_0 + UNITS * (tile + GROUP)))
                if k == PER_ORDER:
                    dve.wait_ge(xin_ready[1], 2 * p + l)
                if k == 0 and l == 1:
                    dve.wait_ge(xin_ready[0], UNITS * (2 * p + 1))
                out, tiles, other = z[:, n % Z_BUFS], rep[:, j, tile:tile + GROUP], xin[order]
                if k == 0 and l == 2:
                    for u in range(UNITS):
                        cols = slice(u * UNIT, (u + 1) * UNIT)
                        dve.wait_ge(xin_ready[0], UNITS * (2 * p + 1) + (u + 1))
                        ins = dve.tensor_tensor(out[:, :, cols], tiles[:, :, cols],
                                                other[:, cols].unsqueeze(1).to_broadcast([P, GROUP, UNIT]), ALU.mult)
                    ins.then_inc(z_ready, 1)
                elif k == GROUPS - 1 and l == 1:
                    for t in range(GROUP):
                        dve.tensor_tensor(out[:, t], tiles[:, t], other[:], ALU.mult).then_inc(z_ready, 1)
                else:
                    dve.tensor_tensor(out, tiles, other[:].unsqueeze(1).to_broadcast([P, GROUP, COLS]),
                                      ALU.mult).then_inc(z_ready, 1)

            def multiply0(b, j):
                p = b * HALVES + j
                dve.wait_ge(slot_copied, p * SLOTS + layer0_slots[1])
                dve.wait_ge(z0_used, p)
                dve.tensor_tensor(*layer0_operands(1), ALU.mult).then_inc(z0_half_ready[1], 1)

            def step_works(b, j):
                for l, k in layers_12:
                    multiply(b, j, l, k)
                    if (l, k) == (1, GROUPS - 1):
                        if j == 0:
                            multiply0(b, 1)
                        else:
                            multiply0(b + 1, 0)

            for j in range(HALVES):
                step_works(0, j)
            with dve.Fori(1, BLOCKS - 1) as b:
                for j in range(HALVES):
                    step_works(b, j)
            step_works(BLOCKS - 1, 0)

            for l, k in layers_12:
                multiply(BLOCKS - 1, 1, l, k)

            r = relu_out[2][:].rearrange("p (i n) -> p i n", i=2)
            dve.wait_ge(relu_used[2], STEPS - 1)
            dve.wait_ge(zsum_step[1], 2 * BLOCKS)
            dve.wait_ge(relu_ready[2], STEPS)
            dve.tensor_tensor(zsum_b[:], r[:, 0], r[:, 1], ALU.add).then_inc(last_added, 1)
            dve.wait_ge(last_added, 1)
            dve.tensor_tensor(zsum_c[:, 2], zsum_a[:, 2], zsum_b[:], ALU.add).then_inc(last_added, 1)
            dve.wait_ge(last_added, 2)
            dve.tensor_tensor(zsum[:, 2, last_rows:ROWS], zsum_c[:, 2, 0:P], zsum_c[:, 2, P:Q],
                              ALU.add).then_inc(last_added, 1)
            pack(dve, slice(last_rows, ROWS), 3, last_packed)


def kernel(**inputs):
    import concourse.bacc as bacc
    from concourse.bass_utils import run_bass_kernel_spmd

    w0 = inputs["L0_rec_W0"]
    m = np.arange(M)
    row, other = layer0_rows()
    arrays = {
        "ids": inputs["ids"],
        "selections": selections(),
        "identity": identity(),
        "w0_mh": w0[row, other],
        "w0_hm": w0[other, row],
        "w0_mm": w0[m, m],
        "w1": by_orders(inputs["L0_rec_W1"]),
        "w2": by_orders(inputs["L0_rec_W2"]),
        "W_top1": inputs["W_top1"],
        "W_top2": inputs["W_top2"],
        "top3": inputs["W_top3"].reshape(F_TOP2 // P, P).T,
        "bias1": inputs["b_top1"].reshape(F_TOP1 // P, P).T,
        "bias2": inputs["b_top2"].reshape(F_TOP2 // P, P).T,
        "ctxT": inputs["dense_ctx"].T,
    }
    arrays.update({f"tbl_{i}": inputs[f"tbl_{i}"] for i in range(M)})
    arrays = {name: np.ascontiguousarray(x) for name, x in arrays.items()}

    nc = bacc.Bacc("TRN2", target_bir_lowering=False, num_devices=1)
    aps = {name: nc.dram_tensor("in_" + name, x.shape, mybir.dt.from_np(x.dtype), kind="ExternalInput").ap()
           for name, x in arrays.items()}
    aps["out"] = nc.dram_tensor("out", (ROWS, 1), F32, kind="ExternalOutput").ap()
    build(nc, aps)
    result = run_bass_kernel_spmd(nc, [{"in_" + name: x for name, x in arrays.items()}], core_ids=[0])
    return result.results[0]["out"]
```
